# Optimizing a Trainium2 kernel written in Bass

```python
import numpy as np
import jax
import jax.numpy as jnp

def _softmax(x, axis=-1):
    return jax.nn.softmax(x, axis=axis)

def _gelu(x):
    return jax.nn.gelu(x, approximate=True)

def _silu(x):
    return jax.nn.silu(x)

def _sigmoid(x):
    return jax.nn.sigmoid(x)

def _layernorm(x, axis=-1, eps=1e-05):
    m = jnp.mean(x, axis=axis, keepdims=True)
    v = jnp.var(x, axis=axis, keepdims=True)
    return (x - m) / jnp.sqrt(v + eps)

def _scatter_add(tgt, idx, src, axis=0):
    return tgt.at[idx].add(src)

def _segment_sum(src, seg, n):
    return jax.ops.segment_sum(src, seg, n)
kernel_name = 'mk_seq_preln_d1_jaxref_r8_fcbb38'

def setup_inputs(seed: int=0):
    np.random.seed(seed)
    _w = jnp.asarray

    def _L0_attn_setup():
        import jax, jax.numpy as jnp
        import numpy as np
        B, N, DIM = (2, 256, 128)
        HEADS, DHEAD = (16, 64)
        GNN_DEPTH = 2
        EPS = 1e-05

        def layer_norm(x, gamma):
            mu = jnp.mean(x, axis=-1, keepdims=True)
            var = jnp.var(x, axis=-1, keepdims=True)
            return (x - mu) / jnp.sqrt(var + EPS) * gamma
        key = jax.random.key(seed)
        ks = jax.random.split(key, 12)
        hd = HEADS * DHEAD
        s = lambda fan: 1.0 / np.sqrt(fan)
        return {'x': jax.random.normal(ks[0], (B, N, DIM), dtype=jnp.float32), 'gamma_in': jnp.ones((DIM,), dtype=jnp.float32), 'Wq': jax.random.normal(ks[1], (DIM, hd), dtype=jnp.float32) * s(DIM), 'Wk': jax.random.normal(ks[2], (DIM, hd), dtype=jnp.float32) * s(DIM), 'Wv': jax.random.normal(ks[3], (DIM, hd), dtype=jnp.float32) * s(DIM), 'gnn_w': jax.random.normal(ks[4], (GNN_DEPTH, DHEAD, DHEAD), dtype=jnp.float32) * s(DHEAD), 'gnn_b': jnp.zeros((GNN_DEPTH, DHEAD), dtype=jnp.float32), 'lin_w': jax.random.normal(ks[5], (DHEAD, DHEAD), dtype=jnp.float32) * s(DHEAD), 'lin_b': jnp.zeros((DHEAD,), dtype=jnp.float32), 'Wo': jax.random.normal(ks[6], (hd, DIM), dtype=jnp.float32) * s(hd), 'gamma_out': jnp.ones((DIM,), dtype=jnp.float32)}
    _L0_attn_in = _L0_attn_setup()

    def _L0_ffn_setup():
        import jax, jax.numpy as jnp
        import numpy as np
        DIM = 128
        HID = 352
        E = 8
        TOP_K = 2
        EPS = 1e-06

        def _rmsnorm(x, w):
            var = jnp.mean(jnp.square(x), axis=-1, keepdims=True)
            return x * jax.lax.rsqrt(var + EPS) * w
        key = jax.random.key(seed)
        ks = jax.random.split(key, 5)
        x = jax.random.normal(ks[0], (4, 256, DIM), dtype=jnp.float32)
        norm_weight = jnp.ones((DIM,), dtype=jnp.float32)
        router_weight = jax.random.normal(ks[1], (E, DIM), dtype=jnp.float32) * 0.02
        gate_up_weight = jax.random.normal(ks[2], (E, 2 * HID, DIM), dtype=jnp.float32) * (0.02 / np.sqrt(E))
        down_weight = jax.random.normal(ks[3], (E, DIM, HID), dtype=jnp.float32) * (0.02 / np.sqrt(E))
        residual_alpha = jnp.float32(1.0)
        return {'x': x, 'norm_weight': norm_weight, 'router_weight': router_weight, 'gate_up_weight': gate_up_weight, 'down_weight': down_weight, 'residual_alpha': residual_alpha}
    _L0_ffn_in = _L0_ffn_setup()
    _d = {'L0_attn_x': _L0_attn_in['x'], 'L0_attn_gamma_in': _L0_attn_in['gamma_in'], 'L0_attn_Wq': _L0_attn_in['Wq'], 'L0_attn_Wk': _L0_attn_in['Wk'], 'L0_attn_Wv': _L0_attn_in['Wv'], 'L0_attn_gnn_w': _L0_attn_in['gnn_w'], 'L0_attn_gnn_b': _L0_attn_in['gnn_b'], 'L0_attn_lin_w': _L0_attn_in['lin_w'], 'L0_attn_lin_b': _L0_attn_in['lin_b'], 'L0_attn_Wo': _L0_attn_in['Wo'], 'L0_attn_gamma_out': _L0_attn_in['gamma_out'], 'L0_ffn_norm_weight': _L0_ffn_in['norm_weight'], 'L0_ffn_router_weight': _L0_ffn_in['router_weight'], 'L0_ffn_gate_up_weight': _L0_ffn_in['gate_up_weight'], 'L0_ffn_down_weight': _L0_ffn_in['down_weight'], 'L0_ffn_residual_alpha': _L0_ffn_in['residual_alpha']}
    _x0 = _d['L0_attn_x']
    _d['L0_attn_x'] = jax.random.normal(jax.random.fold_in(jax.random.key(seed), 1), (16, 256, 128), dtype=_x0.dtype)
    del _x0
    return _d

def reference(L0_attn_x, L0_attn_gamma_in, L0_attn_Wq, L0_attn_Wk, L0_attn_Wv, L0_attn_gnn_w, L0_attn_gnn_b, L0_attn_lin_w, L0_attn_lin_b, L0_attn_Wo, L0_attn_gamma_out, L0_ffn_norm_weight, L0_ffn_router_weight, L0_ffn_gate_up_weight, L0_ffn_down_weight, L0_ffn_residual_alpha):

    def _L0_attn_ref(x, gamma_in, Wq, Wk, Wv, gnn_w, gnn_b, lin_w, lin_b, Wo, gamma_out):
        import jax, jax.numpy as jnp
        import numpy as np
        B, N, DIM = (2, 256, 128)
        HEADS, DHEAD = (16, 64)
        GNN_DEPTH = 2
        EPS = 1e-05

        def layer_norm(x, gamma):
            mu = jnp.mean(x, axis=-1, keepdims=True)
            var = jnp.var(x, axis=-1, keepdims=True)
            return (x - mu) / jnp.sqrt(var + EPS) * gamma
        b, n, _ = x.shape
        scale = DHEAD ** (-0.5)
        xn = layer_norm(x, gamma_in)
        q = (xn @ Wq).reshape(b, n, HEADS, DHEAD).transpose(0, 2, 1, 3) * scale
        k = (xn @ Wk).reshape(b, n, HEADS, DHEAD).transpose(0, 2, 1, 3)
        v = (xn @ Wv).reshape(b, n, HEADS, DHEAD).transpose(0, 2, 1, 3)
        sim = jnp.einsum('bhid,bhjd->bhij', q, k)
        mask_value = -jnp.finfo(sim.dtype).max
        causal_mask = jnp.triu(jnp.ones((n, n), dtype=bool), k=1)
        sim = jnp.where(causal_mask, mask_value, sim)
        attn = jax.nn.softmax(sim.astype(jnp.float32), axis=-1)
        out = jnp.einsum('bhij,bhjd->bhid', attn, v)
        adj = attn.reshape(b * HEADS, n, n)
        adj = jnp.clip(adj + jnp.eye(n, dtype=adj.dtype), 0.0, 1.0)
        deg = jnp.sum(adj, axis=-1, keepdims=True)
        feats = v.reshape(b * HEADS, n, DHEAD)
        for l in range(GNN_DEPTH):
            h = feats @ gnn_w[l] + gnn_b[l]
            h = jnp.einsum('bij,bjd->bid', adj, h) / deg
            feats = jax.nn.gelu(h + feats, approximate=False)
        gnn_out = feats @ lin_w + lin_b
        out = out + gnn_out.reshape(b, HEADS, n, DHEAD)
        out = out.transpose(0, 2, 1, 3).reshape(b, n, HEADS * DHEAD)
        return layer_norm(out @ Wo, gamma_out)

    def _L0_ffn_ref(x, norm_weight, router_weight, gate_up_weight, down_weight, residual_alpha):
        import jax, jax.numpy as jnp
        import numpy as np
        DIM = 128
        HID = 352
        E = 8
        TOP_K = 2
        EPS = 1e-06

        def _rmsnorm(x, w):
            var = jnp.mean(jnp.square(x), axis=-1, keepdims=True)
            return x * jax.lax.rsqrt(var + EPS) * w
        normed = _rmsnorm(x, norm_weight)
        logits = jnp.einsum('bsd,ed->bse', normed, router_weight)
        probs = jax.nn.softmax(logits, axis=-1)
        topk_w, topk_idx = jax.lax.top_k(probs, TOP_K)
        topk_w = topk_w / jnp.sum(topk_w, axis=-1, keepdims=True)
        combine = jnp.sum(jax.nn.one_hot(topk_idx, E, dtype=normed.dtype) * topk_w[..., None], axis=-2)
        moe_out = jnp.zeros_like(x)
        for e in range(E):
            gu = jnp.einsum('bsd,hd->bsh', normed, gate_up_weight[e])
            gate, up = (gu[..., :HID], gu[..., HID:])
            hidden = jax.nn.silu(gate) * up
            out_e = jnp.einsum('bsh,dh->bsd', hidden, down_weight[e])
            moe_out = moe_out + combine[..., e, None] * out_e
        alpha = jnp.clip(residual_alpha, -0.5, 2.0)
        return x + alpha * moe_out
    x = L0_attn_x
    x = x + _L0_attn_ref(_layernorm(x, axis=-1), L0_attn_gamma_in, L0_attn_Wq, L0_attn_Wk, L0_attn_Wv, L0_attn_gnn_w, L0_attn_gnn_b, L0_attn_lin_w, L0_attn_lin_b, L0_attn_Wo, L0_attn_gamma_out)
    x = x + _L0_ffn_ref(_layernorm(x, axis=-1), L0_ffn_norm_weight, L0_ffn_router_weight, L0_ffn_gate_up_weight, L0_ffn_down_weight, L0_ffn_residual_alpha)
    return x

_drawn_inputs = setup_inputs


def setup_inputs(seed=0):
    import zlib

    import numpy as np

    out = dict(_drawn_inputs(seed))
    spreads = {'L0_attn_gamma_in': (1.0, 0.2),
     'L0_attn_gnn_b': (0.0, 0.1),
     'L0_attn_lin_b': (0.0, 0.1),
     'L0_attn_gamma_out': (1.0, 0.2),
     'L0_ffn_norm_weight': (1.0, 0.6)}
    factors = {'L0_ffn_router_weight': 8.0, 'L0_ffn_gate_up_weight': 8.0, 'L0_ffn_down_weight': 8.0}
    for name, (base, spread) in spreads.items():
        noise = np.random.default_rng([zlib.crc32(name.encode()), seed]).standard_normal(out[name].shape)
        drawn = base * np.exp(spread * noise) if base else spread * noise
        out[name] = jnp.asarray(drawn.astype(out[name].dtype))
    for name, factor in factors.items():
        out[name] = (out[name] * factor).astype(out[name].dtype)
    return out
```

```python
from contextlib import ExitStack

import concourse.bass as bass
from concourse import mybir

P = 128
BATCHES, TOKENS, DIM = 16, 256, 128
HEADS, DHEAD = 16, 64
PAIRS = HEADS // 2
TILES = TOKENS // P
HD = HEADS * DHEAD
ALL = BATCHES * TOKENS
EXPERTS, HID = 8, 352
BLOCK = 512
BLOCKS, BT = ALL // BLOCK, BLOCK // P
CHUNKS = [(c, min(P, HID - c)) for c in range(0, HID, P)]
NC = len(CHUNKS)
EPS_LN, EPS_RMS = 1e-5, 1e-6
MASKED = -3.0e38
SCALE = DHEAD ** -0.5

f32, f32r, bf16, u32 = mybir.dt.float32, mybir.dt.float32r, mybir.dt.bfloat16, mybir.dt.uint32
ALU = mybir.AluOpType
ACT = mybir.ActivationFunctionType
X = mybir.AxisListType.X


class Signal:

    def __init__(self, sem, per):
        self.sem, self.per = sem, per

    def wait(self, engine, turn, k):
        engine.wait_ge(self.sem, turn * self.per + k)


def build_program(nc, x, wq, wk, wv, wvT, gnn_w, gnn_b, lin_wT, lin_b, wo, gamma_in, gamma_out,
                  norm_w, routerT, guT, downT, alpha, out):
    ctx = ExitStack()
    attn = ExitStack()

    def sb(name, shape, dt=f32, where=ctx):
        return where.enter_context(nc.sbuf_tensor(name, shape, dt))

    def sem(name):
        return ctx.enter_context(nc.semaphore(name))

    with ctx:
        bank = [ctx.enter_context(nc.psum_tensor(f"bank{i}", [P, 512], f32)) for i in range(8)]

        x_all = sb("x_all", [P, BATCHES * TILES, DIM])
        y_all = sb("y_all", [P, BATCHES * TILES, DIM])
        ident = sb("ident", [P, P])
        half = sb("half", [P, BT])
        gout = sb("gout", [P, DIM])
        normw = sb("normw", [P, 1])
        hold = sb("hold", [P, 1])
        rtT = sb("rtT", [P, EXPERTS])
        alph = sb("alph", [P, 1])

        def at(name, shape, dt=f32):
            return sb(name, shape, dt, attn)

        raw = at("raw", [P, 3, HD])
        wvt = at("wvt", [P, PAIRS, P])
        wo_sb = at("wo_sb", [P, PAIRS, P])
        gw = at("gw", [P, 2, P])
        gwi = at("gwi", [P, P])
        linT = at("linT", [P, P])
        gb = at("gb", [P, 2])
        lb = at("lb", [P, 1])
        gin = at("gin", [P, 1])
        w_hi = at("w_hi", [P, 3, HD], f32r)
        w_lo = at("w_lo", [P, 3, HD], f32r)
        v_hi = at("v_hi", [P, HD], f32r)
        v_lo = at("v_lo", [P, HD], f32r)
        mv_hi = at("mv_hi", [P, HD], f32r)
        mv_lo = at("mv_lo", [P, HD], f32r)
        cy_hi = at("cy_hi", [P, P], f32r)
        cy_lo = at("cy_lo", [P, P], f32r)
        lwo = at("lwo", [P, PAIRS, P])
        yb = at("yb", [P, 1])
        ident_bf = at("ident_bf", [P, P], bf16)
        maskf = at("maskf", [P, P])
        mask = at("mask", [P, 2, P], bf16)
        idw = at("idw", [P, 2 * P])
        stat = at("stat", [P, TILES, 6])
        mv_ = at("mv_", [P, TILES, 2])
        ve = at("ve", [P, TILES])
        rstd = at("rstd", [P, TILES])
        xh = at("xh", [P, TILES, DIM])
        xn = at("xn", [P, TILES, DIM])
        xt_hi = at("xt_hi", [P, TOKENS], f32r)
        xt_lo = at("xt_lo", [P, TOKENS], f32r)
        vnat = at("vnat", [P, TILES, HD])
        qT = at("qT", [P, 2, TOKENS])
        kT = at("kT", [P, 2, 2, TOKENS])
        nmax = at("nmax", [P, 3, 4])
        ssum = at("ssum", [P, 3, 4])
        den = at("den", [P, 3, 4])
        rs = at("rs", [P, 3, 4])
        wgt = at("wgt", [P, 3, 4])
        deg = at("deg", [P, 3, 4, DHEAD])
        ea = at("ea", [P, 3, 2, P])
        eb = at("eb", [P, 3, 2, 2 * P])
        gt0 = at("gt0", [P, PAIRS, 2, TOKENS])
        gt1 = at("gt1", [P, PAIRS, 2, P])
        dT = at("dT", [P, PAIRS, TOKENS])
        aT = at("aT", [P, PAIRS, TOKENS])
        f1T = at("f1T", [P, 4, TOKENS])
        g1 = at("g1", [P, 2, TILES, P])
        z2 = at("z2", [P, 2, TOKENS])
        f2T = at("f2T", [P, 2, TOKENS])
        yT = at("yT", [P, TOKENS])
        attn.close()

        raw_gu = sb("raw_gu", [P, 2, 2 * HID])
        gu_hi = sb("gu_hi", [P, EXPERTS, 2 * HID], f32r)
        gu_lo = sb("gu_lo", [P, EXPERTS, 2 * HID], f32r)
        dn = sb("dn", [P, EXPERTS, NC, DIM])
        zt_hi = sb("zt_hi", [P, ALL], f32r)
        zt_lo = sb("zt_lo", [P, ALL], f32r)
        zT = sb("zT", [P, BLOCK])
        st4 = sb("st4", [P, BT, 6])
        mv4 = sb("mv4", [P, BT, 2])
        ve4 = sb("ve4", [P, BT])
        rs4 = sb("rs4", [P, BT])
        t4 = sb("t4", [P, BT, DIM])
        z4 = sb("z4", [P, BT, DIM])
        sq4 = sb("sq4", [P, BT, DIM])
        ss4 = sb("ss4", [P, BT])
        lg = sb("lg", [P, BT, EXPERTS])
        top = sb("top", [P, BT, 8])
        topi = sb("topi", [P, BT, 8], u32)
        topf = sb("topf", [P, BT, 2])
        iot = sb("iot", [P, EXPERTS])
        gap = sb("gap", [P, BT])
        th = sb("th", [P, BT])
        wt2 = sb("wt2", [P, 2, BT])
        eq = sb("eq", [P, 2, BT, EXPERTS])
        comb = sb("comb", [P, BLOCKS, BT, EXPERTS])
        sg = sb("sg", [P, 2, BLOCK])
        hT = sb("hT", [P, 2, NC, BLOCK])
        acc = sb("acc", [P, 2, BT, DIM])

        w_x0, w_x, w_w, w_small = sem("w_x0"), sem("w_x"), sem("w_w"), sem("w_small")
        w_gu = [sem(f"w_gu{i}") for i in range(2)]
        w_dn = [sem(f"w_dn{e}") for e in range(EXPERTS)]
        k_pool, k_dve, k_pe, k_act = sem("k_pool"), sem("k_dve"), sem("k_pe"), sem("k_act")
        d_ln = Signal(sem("d_ln"), 8)
        p_ln = Signal(sem("p_ln"), 2)
        s_xt = Signal(sem("s_xt"), 1)
        a_xt = Signal(sem("a_xt"), 1)
        d_xt = Signal(sem("d_xt"), 1)
        s_v = Signal(sem("s_v"), 4)
        a_v = Signal(sem("a_v"), 4)
        s_qk, a_qk = Signal(sem("s_qk"), PAIRS), Signal(sem("a_qk"), PAIRS)
        s_s = Signal(sem("s_s"), 2 * PAIRS)
        d_max = Signal(sem("d_max"), 2 * PAIRS)
        a_exp = Signal(sem("a_exp"), 2 * PAIRS)
        d_e = Signal(sem("d_e"), PAIRS)
        d_w = Signal(sem("d_w"), PAIRS)
        p_deg = Signal(sem("p_deg"), PAIRS)
        p_g = Signal(sem("p_g"), PAIRS)
        s_t, a_gt = Signal(sem("s_t"), PAIRS), Signal(sem("a_gt"), PAIRS)
        s_d, a_d = Signal(sem("s_d"), PAIRS), Signal(sem("a_d"), PAIRS)
        s_deg = Signal(sem("s_deg"), PAIRS)
        d_a = Signal(sem("d_a"), PAIRS)
        s_f1, a_f1 = Signal(sem("s_f1"), PAIRS), Signal(sem("a_f1"), PAIRS)
        s_g1, d_g1 = Signal(sem("s_g1"), PAIRS), Signal(sem("d_g1"), PAIRS)
        s_h2, d_z2 = Signal(sem("s_h2"), PAIRS), Signal(sem("d_z2"), PAIRS)
        a_f2 = Signal(sem("a_f2"), PAIRS)
        s_y, d_yT = Signal(sem("s_y"), 1), Signal(sem("d_yT"), 1)
        s_yn, d_y = Signal(sem("s_yn"), 1), Signal(sem("d_y"), 1)
        d_st = Signal(sem("d_st"), 24)
        p_st = Signal(sem("p_st"), 3)
        s_zt, a_zt, d_zl = Signal(sem("s_zt"), 1), Signal(sem("a_zt"), 1), Signal(sem("d_zl"), 1)
        s_lg, a_th, d_comb = Signal(sem("s_lg"), 1), Signal(sem("a_th"), 1), Signal(sem("d_comb"), 1)
        k_gu = sem("k_gu")
        s_gt = Signal(sem("s_gt"), EXPERTS * NC)
        s_up = Signal(sem("s_up"), EXPERTS * NC)
        a_sg = Signal(sem("a_sg"), EXPERTS * NC)
        d_h = Signal(sem("d_h"), EXPERTS * NC)
        s_dn = Signal(sem("s_dn"), EXPERTS)
        d_acc = Signal(sem("d_acc"), EXPERTS)
        o_out = [Signal(sem(f"o_out{i}"), 16) for i in range(2)]

        def xt(t):
            return slice(t * P, (t + 1) * P)

        def tokens(b):
            return bass.ds(b * TILES, TILES)

        block = ctx.enter_context(nc.Block())

        @block.sync
        def _(sp):
            xv = x.rearrange("(t p) d -> p t d", p=P)
            sp.dma_start(x_all[:, 0:TILES, :], xv[:, 0:TILES, :]).then_inc(w_x0, 16)
            for dst, src in ((gin[:, :], gamma_in), (normw[:, :], norm_w), (rtT[:, :], routerT),
                             (gout[:, :], gamma_out.to_broadcast([P, DIM])),
                             (alph[:, :], alpha.to_broadcast([P, 1]))):
                sp.dma_start(dst, src).then_inc(w_small, 16)
            for n, w in enumerate((wq, wk, wv)):
                sp.dma_start(raw[:, n, :], w).then_inc(w_w, 16)
            sp.dma_start(wvt[:, :, :], wvT.rearrange("(g p) d -> p g d", p=P)).then_inc(w_w, 16)
            sp.dma_start(wo_sb[:, :, :], wo.rearrange("(g p) d -> p g d", p=P)).then_inc(w_w, 16)
            sp.wait_ge(k_pool, 1)
            for h in range(2):
                at_ = slice(h * DHEAD, (h + 1) * DHEAD)
                for l in range(2):
                    sp.dma_start(gw[at_, l, at_], gnn_w[l]).then_inc(w_small, 16)
                    sp.dma_start(gb[at_, l:l + 1], gnn_b[l:l + 1, :].rearrange("o d -> d o")).then_inc(w_small, 16)
                sp.dma_start(linT[at_, at_], lin_wT).then_inc(w_small, 16)
                sp.dma_start(lb[at_, :], lin_b).then_inc(w_small, 16)
            sp.dma_start(x_all[:, TILES:, :], xv[:, TILES:, :]).then_inc(w_x, 16)

            d_y.wait(sp, BATCHES - 1, 1)
            for e in range(EXPERTS):
                if e >= 2:
                    sp.wait_ge(k_gu, 2 * (e - 1))
                sp.dma_start(raw_gu[:, e % 2, :], guT[e]).then_inc(w_gu[e % 2], 16)
                for c, (at_, n) in enumerate(CHUNKS):
                    sp.dma_start(dn[0:n, e, c, :], downT[e, at_:at_ + n, :]).then_inc(w_dn[e], 16)
            ov = out.rearrange("(k t p) d -> k p t d", p=P, t=BT)
            with sp.Fori(0, BLOCKS // 2) as i:
                for half_ in range(2):
                    k = i * 2 + half_
                    d_acc.wait(sp, k, EXPERTS)
                    sp.dma_start(ov[bass.ds(k, 1), :, :, :].rearrange("o p t d -> p (o t) d"),
                                 acc[:, half_, :, :]).then_inc(o_out[half_].sem, 16)
            for done in o_out:
                done.wait(sp, BLOCKS // 2, 0)

        SMALL_ALL = 17 * 16
        POWERS = (3, 9, 13)
        NORMED, SPLIT, GAP, CHOSEN, ROUTED = 14, 15, 18, 21, 24

        @block.gpsimd
        def _(pool):
            nc.gpsimd.memset(gw[:, :, :], 0.0)
            nc.gpsimd.memset(linT[:, :], 0.0).then_inc(k_pool, 1)
            nc.gpsimd.memset(half[:, :], -0.5)
            nc.gpsimd.memset(ident[:, :], 0.0)
            nc.gpsimd.memset(idw[:, :], 0.0)
            nc.gpsimd.memset(maskf[:, :], 0.0)
            nc.gpsimd.memset(kT[:, :, :, :], 0.0).then_inc(k_pool, 1)
            pool.wait_ge(k_pool, 2)
            for m in (ident[:, :], idw[:, P:2 * P]):
                nc.gpsimd.affine_select(out=m, in_=m, compare_op=ALU.not_equal, fill=1.0,
                                        base=0, pattern=[[-1, P]], channel_multiplier=1)
            nc.gpsimd.affine_select(out=maskf[:, :], in_=maskf[:, :], compare_op=ALU.is_ge, fill=MASKED,
                                    base=0, pattern=[[-1, P]], channel_multiplier=1).then_inc(k_pool, 1)

            def deviation(b, step, d_step):
                d_ln.wait(pool, b, d_step)
                nc.gpsimd.tensor_tensor(rstd[:, :], ve[:, :], half[:, 0:TILES], ALU.pow).then_inc(p_ln.sem, 1)

            def graph(b, n):
                s = n % 3
                d_w.wait(pool, b, n + 1)
                nc.gpsimd.tensor_tensor(ea[:, s], ea[:, s],
                                        wgt[:, s, 0:2].unsqueeze(2).to_broadcast([P, 2, P]), ALU.mult)
                nc.gpsimd.tensor_tensor(eb[:, s], eb[:, s],
                                        wgt[:, s, 2:4].unsqueeze(2).to_broadcast([P, 2, 2 * P]),
                                        ALU.mult).then_inc(p_g.sem, 1)
                nc.gpsimd.tensor_tensor(deg[:, s], den[:, s, :].unsqueeze(2).to_broadcast([P, 4, DHEAD]),
                                        rs[:, s, :].unsqueeze(2).to_broadcast([P, 4, DHEAD]),
                                        ALU.mult).then_inc(p_deg.sem, 1)

            deviation(0, 0, 3)
            deviation(0, 1, 7)
            for n in range(PAIRS):
                graph(0, n)
            with pool.Fori(0, BATCHES - 1) as b:
                deviation(b + 1, 0, 3)
                deviation(b + 1, 1, 7)
                for n in range(PAIRS):
                    graph(b + 1, n)

            def prepare(k):
                for i, step in enumerate(POWERS):
                    d_st.wait(pool, k, step)
                    nc.gpsimd.tensor_tensor(rs4[:, :], ve4[:, :], half[:, :], ALU.pow).then_inc(p_st.sem, 1)

            d_y.wait(pool, BATCHES - 1, 1)
            nc.gpsimd.iota(iot[:, :], pattern=[[1, EXPERTS]], base=0, channel_multiplier=0,
                           allow_small_or_imprecise_dtypes=True).then_inc(k_pool, 1)
            prepare(0)
            with pool.Fori(0, BLOCKS - 1) as k:
                prepare(k + 1)

        @block.tensor
        def _(pe):
            def product(o, st, mo, first, last, **more):
                nc_mm = nc.tensor.matmul
                return nc_mm(o, st, mo, start=first, stop=last, **more)

            def product3(o, st_hi, st_lo, mo_hi, mo_lo, first=True, last=True, **more):
                product(o, st_hi, mo_lo, first, False, **more)
                product(o, st_lo, mo_hi, False, False, **more)
                return product(o, st_hi, mo_hi, False, last, **more)

            def prepare_weights():
                pe.wait_ge(k_pool, 3)
                pe.wait_ge(w_w, 5 * 16)
                pe.wait_ge(w_small, SMALL_ALL)
                pe.wait_ge(k_dve, 1)
                for g in range(PAIRS):
                    mm = product(bank[g // 4][:, (g % 4) * P:(g % 4 + 1) * P], wvt[:, g, :], gwi[:, :], True, True)
                mm.then_inc(k_pe, 1)
                for g in range(PAIRS):
                    mm = product(bank[2 + g // 4][:, (g % 4) * P:(g % 4 + 1) * P], linT[:, :], wo_sb[:, g, :], True, True)
                mm.then_inc(k_pe, 1)
                for g in range(PAIRS):
                    mm = product(bank[4][:, 0:P], wvt[:, g, :], wo_sb[:, g, :], g == 0, g == PAIRS - 1)
                for g in range(PAIRS):
                    mm = product(bank[5][:, 0:1], wo_sb[:, g, :], lb[:, :], g == 0, g == PAIRS - 1)
                mm.then_inc(k_pe, 1)

            def x_transposed(b):
                d_ln.wait(pe, b, 8)
                for t in range(TILES):
                    mm = nc.tensor.transpose(bank[6][:, xt(t)], xn[:, t, :], ident[:, :])
                mm.then_inc(s_xt.sem, 1)

            def values(b, c):
                t, h = c // 2, c % 2
                if c == 0:
                    a_xt.wait(pe, b, 1)
                    d_xt.wait(pe, b, 1)
                if c >= 2:
                    a_v.wait(pe, b, c - 1)
                cols = slice(h * 512, (h + 1) * 512)
                product3(bank[c % 2][:, :], xt_hi[:, xt(t)], xt_lo[:, xt(t)],
                         v_hi[:, cols], v_lo[:, cols]).then_inc(s_v.sem, 1)

            def queries_keys(b, n):
                if n == 0:
                    a_v.wait(pe, b, 3)
                else:
                    a_qk.wait(pe, b, n)
                cols = slice(n * P, (n + 1) * P)
                product3(bank[0][:, 0:TOKENS], w_hi[:, 0, cols], w_lo[:, 0, cols], xt_hi[:, :], xt_lo[:, :])
                product3(bank[0][:, TOKENS:], w_hi[:, 1, cols], w_lo[:, 1, cols],
                         xt_hi[:, :], xt_lo[:, :]).then_inc(s_qk.sem, 1)

            def scores(b, n):
                a_qk.wait(pe, b, n + 1)
                if n == 0:
                    a_v.wait(pe, b, 4)
                else:
                    a_exp.wait(pe, b, 2 * n - 1)
                q, k = qT[:, n % 2], kT[:, n % 2]
                product(bank[1][:, 0:2 * P], ident_bf[:, :], mask[:, :, :], True, False)
                product(bank[1][:, 0:2 * P], q[:, xt(0)], k[:, :, xt(0)], False, True).then_inc(s_s.sem, 1)
                if n >= 1:
                    a_exp.wait(pe, b, 2 * n)
                sb1 = bank[2][:, :].rearrange("p (h j) -> p h j", h=2)
                product(sb1[:, :, xt(1)], ident_bf[:, :], mask[:, :, :], True, False, skip_group_check=True)
                product(bank[2][:, :], q[:, xt(1)], k[:, :, :], False, True,
                        skip_group_check=True).then_inc(s_s.sem, 1)

            def transposes(b, n):
                s = n % 3
                p_g.wait(pe, b, n + 1)
                if n >= 1:
                    a_gt.wait(pe, b, n)
                for a in range(2):
                    nc.tensor.transpose(bank[3][:, a * TOKENS:a * TOKENS + P], ea[:, s, a, :], ident[:, :])
                    nc.tensor.transpose(bank[3][:, a * TOKENS + P:(a + 1) * TOKENS], eb[:, s, a, 0:P], ident[:, :])
                for a in range(2):
                    mm = nc.tensor.transpose(bank[4][:, a * P:(a + 1) * P], eb[:, s, a, P:], ident[:, :])
                mm.then_inc(s_t.sem, 1)

            def mixed(o, left, n):
                for tile, moving, cols in ((0, gt0, slice(0, TOKENS)), (1, gt1, slice(P, TOKENS))):
                    for a in range(2):
                        rows = slice(a * DHEAD, (a + 1) * DHEAD)
                        mm = product(o[rows, cols], left(tile, a), moving[:, n, a, :], tile == 0,
                                     tile == 1, skip_group_check=True)
                return mm

            def differences(b, n):
                a_gt.wait(pe, b, n + 1)
                if n == 0:
                    a_v.wait(pe, b, 4)
                else:
                    a_d.wait(pe, b, n)
                o = bank[5][:, 0:TOKENS]
                mixed(o, lambda t, a: vnat[:, t, n * P + a * DHEAD:n * P + (a + 1) * DHEAD], n)
                cols = slice(n * P, (n + 1) * P)
                product3(o, w_hi[:, 2, cols], w_lo[:, 2, cols], xt_hi[:, :], xt_lo[:, :], first=False,
                         skip_group_check=True).then_inc(s_d.sem, 1)

            def degrees(b, n):
                p_deg.wait(pe, b, n + 1)
                if n >= 1:
                    d_a.wait(pe, b, n)
                for t in range(TILES):
                    mm = nc.tensor.transpose(
                        bank[6][:, xt(t)],
                        deg[:, n % 3, 2 * t:2 * t + 2, :].rearrange("p a c -> p (a c)"), ident[:, :])
                mm.then_inc(s_deg.sem, 1)

            def output_natural(b):
                d_yT.wait(pe, b, 1)
                for t in range(TILES):
                    mm = nc.tensor.transpose(bank[7][:, xt(t)], yT[:, xt(t)], ident[:, :])
                mm.then_inc(s_yn.sem, 1)

            def phase1(b, before):
                queries_keys(b, 0)
                for n in range(PAIRS + 2):
                    if n < PAIRS:
                        scores(b, n)
                    if n >= 2:
                        transposes(b, n - 2)
                    if n + 1 < PAIRS:
                        queries_keys(b, n + 1)
                    if n >= 2:
                        differences(b, n - 2)
                        degrees(b, n - 2)
                    if n == 1 and before is not None:
                        output_natural(before)

            def layer1(b, n):
                if n == 0:
                    a_d.wait(pe, b, PAIRS)
                if n >= 2:
                    a_f1.wait(pe, b, n - 1)
                o = bank[n % 2][:, 0:TOKENS]
                product(o, gw[:, 0, :], dT[:, n, :], True, False)
                cols = slice(n * P, (n + 1) * P)
                product3(o, mv_hi[:, cols], mv_lo[:, cols], xt_hi[:, :], xt_lo[:, :],
                         first=False).then_inc(s_f1.sem, 1)

            def layer2_in(b, n):
                a_f1.wait(pe, b, n + 1)
                if n >= 2:
                    d_g1.wait(pe, b, n - 1)
                for t in range(TILES):
                    mm = product(bank[2 + n % 2][:, xt(t)], f1T[:, n % 4, xt(t)], gw[:, 1, :], True, True)
                mm.then_inc(s_g1.sem, 1)

            def layer2(b, n):
                d_g1.wait(pe, b, n + 1)
                if n >= 2:
                    d_z2.wait(pe, b, n - 1)
                mixed(bank[4 + n % 2][:, 0:TOKENS],
                      lambda t, a: g1[:, n % 2, t, a * DHEAD:(a + 1) * DHEAD], n).then_inc(s_h2.sem, 1)

            def output_start(b):
                product3(bank[7][:, 0:TOKENS], cy_hi[:, :], cy_lo[:, :], xt_hi[:, :], xt_lo[:, :], last=False)

            def output_part(b, n):
                if n == 0:
                    d_a.wait(pe, b, PAIRS)
                product(bank[7][:, 0:TOKENS], wo_sb[:, n, :], aT[:, n, :], False, False)
                a_f2.wait(pe, b, n + 1)
                mm = product(bank[7][:, 0:TOKENS], lwo[:, n, :], f2T[:, n % 2, :], False, n == PAIRS - 1)
                if n == PAIRS - 1:
                    mm.then_inc(s_y.sem, 1)

            def phase2(b, before, after):
                if before is not None:
                    d_y.wait(pe, before, 1)
                output_start(b)
                for n in range(PAIRS + 3):
                    if n < PAIRS:
                        layer1(b, n)
                    if 0 <= n - 1 < PAIRS:
                        layer2_in(b, n - 1)
                    if 0 <= n - 2 < PAIRS:
                        layer2(b, n - 2)
                    if 0 <= n - 3 < PAIRS:
                        output_part(b, n - 3)
                    if after is not None:
                        if n == 7:
                            d_a.wait(pe, b, PAIRS)
                            x_transposed(after)
                        if n == 9:
                            a_f1.wait(pe, b, PAIRS)
                            values(after, 0)
                            values(after, 1)
                        if n == 10:
                            values(after, 2)
                            values(after, 3)

            prepare_weights()
            x_transposed(0)
            pe.wait_ge(k_dve, 8)
            for c in range(4):
                values(0, c)
            phase1(0, None)
            with pe.Fori(0, BATCHES - 2) as b:
                phase2(b, None, b + 1)
                phase1(b + 1, b)
            phase2(BATCHES - 2, None, BATCHES - 1)
            phase1(BATCHES - 1, BATCHES - 2)
            phase2(BATCHES - 1, None, None)
            output_natural(BATCHES - 1)

            def block_transposed(k):
                d_st.wait(pe, k, NORMED)
                for t in range(BT):
                    mm = nc.tensor.transpose(bank[6][:, xt(t)], z4[:, t, :], ident[:, :])
                mm.then_inc(s_zt.sem, 1)

            def logits(k):
                a_zt.wait(pe, k, 1)
                for t in range(BT):
                    mm = product(bank[7][:, t * EXPERTS:(t + 1) * EXPERTS], zT[:, xt(t)], rtT[:, :], True, True)
                mm.then_inc(s_lg.sem, 1)

            def gate_up(k, e, c):
                i = e * NC + c
                at_, n = CHUNKS[c]
                for part, o, done in ((0, bank[i % 2], s_gt), (1, bank[2 + i % 2], s_up)):
                    cols = slice(part * HID + at_, part * HID + at_ + n)
                    if part == 0 and i >= 2:
                        a_sg.wait(pe, k, i - 1)
                    if part == 1 and i >= 2:
                        d_h.wait(pe, k, i - 1)
                    now = bass.ds(k * BLOCK, BLOCK)
                    product3(o[0:n, :], gu_hi[:, e, cols], gu_lo[:, e, cols],
                             zt_hi[:, now], zt_lo[:, now]).then_inc(done.sem, 1)

            def down(k, e):
                d_h.wait(pe, k, (e + 1) * NC)
                if e >= 2:
                    d_acc.wait(pe, k, e - 1)
                for t in range(BT):
                    for c, (_, n) in enumerate(CHUNKS):
                        mm = product(bank[4 + e % 2][:, xt(t)], hT[0:n, e % 2, c, xt(t)], dn[0:n, e, c, :],
                                     c == 0, c == NC - 1)
                mm.then_inc(s_dn.sem, 1)

            def experts(k, first, after):
                a_zt.wait(pe, k, 1)
                d_zl.wait(pe, k, 1)
                for e in range(EXPERTS):
                    if first:
                        pe.wait_ge(k_gu, 2 * (e + 1))
                        pe.wait_ge(w_dn[e], 16 * NC)
                    for c in range(NC):
                        gate_up(k, e, c)
                        if c == 0 and e >= 1:
                            down(k, e - 1)
                    if e == 3 and after is not None:
                        block_transposed(after)
                    if e == 4 and after is not None:
                        logits(after)
                down(k, EXPERTS - 1)

            block_transposed(0)
            logits(0)
            experts(0, True, 1)
            with pe.Fori(1, BLOCKS - 1) as k:
                experts(k, False, k + 1)
            experts(BLOCKS - 1, False, None)

        @block.scalar
        def _(act):
            def copy(o, i, **more):
                return nc.scalar.activation(o, i, ACT.Copy, **more)

            def prepare_weights():
                act.wait_ge(k_pe, 2)
                copy(lwo[:, 0:4, :], bank[2][:, :].rearrange("p (g n) -> p g n", g=4))
                copy(lwo[:, 4:8, :], bank[3][:, :].rearrange("p (g n) -> p g n", g=4))
                act.wait_ge(k_pe, 3)
                copy(yb[:, :], bank[5][:, 0:1]).then_inc(k_act, 1)

            def x_high(b, earlier):
                s_xt.wait(act, b, 1)
                if earlier is not None:
                    s_f1.wait(act, earlier, PAIRS)
                copy(xt_hi[:, :], bank[6][:, 0:TOKENS], scale=gin[:, :]).then_inc(a_xt.sem, 1)

            def values(b, c):
                s_v.wait(act, b, c + 1)
                t, h = c // 2, c % 2
                copy(vnat[:, t, h * 512:(h + 1) * 512], bank[c % 2][:, :]).then_inc(a_v.sem, 1)

            def queries_keys(b, n):
                s_qk.wait(act, b, n + 1)
                copy(qT[:, n % 2, :], bank[0][:, 0:TOKENS])
                for a in range(2):
                    rows = slice(a * DHEAD, (a + 1) * DHEAD)
                    done = copy(kT[rows, n % 2, a, :], bank[0][rows, TOKENS:], scale=SCALE)
                done.then_inc(a_qk.sem, 1)

            def exps(b, n, t):
                d_max.wait(act, b, 2 * n + 1 + t)
                s, width = n % 3, (t + 1) * P
                e = eb if t else ea
                for a in range(2):
                    i = 2 * t + a
                    done = nc.scalar.activation(e[:, s, a, :], bank[1 + t][:, a * width:(a + 1) * width], ACT.Exp,
                                                bias=nmax[:, s, i:i + 1], accum_out=ssum[:, s, i:i + 1])
                done.then_inc(a_exp.sem, 1)

            def graph(b, n):
                s_t.wait(act, b, n + 1)
                copy(gt0[:, n, :, :], bank[3][:, :].rearrange("p (a i) -> p a i", a=2))
                copy(gt1[:, n, :, :], bank[4][:, 0:2 * P].rearrange("p (a i) -> p a i", a=2)).then_inc(a_gt.sem, 1)

            def differences(b, n):
                s_d.wait(act, b, n + 1)
                copy(dT[:, n, :], bank[5][:, 0:TOKENS]).then_inc(a_d.sem, 1)

            def phase1(b):
                queries_keys(b, 0)
                for n in range(PAIRS + 2):
                    if n < PAIRS:
                        exps(b, n, 0)
                    if n >= 2:
                        graph(b, n - 2)
                    if n < PAIRS:
                        exps(b, n, 1)
                    if n + 1 < PAIRS:
                        queries_keys(b, n + 1)
                    if n >= 2:
                        differences(b, n - 2)

            def gelu1(b, n):
                s_f1.wait(act, b, n + 1)
                nc.scalar.activation(f1T[:, n % 4, :], bank[n % 2][:, 0:TOKENS], ACT.Gelu,
                                     bias=gb[:, 0:1]).then_inc(a_f1.sem, 1)

            def gelu2(b, n):
                d_z2.wait(act, b, n + 1)
                nc.scalar.activation(f2T[:, n % 2, :], z2[:, n % 2, :], ACT.Gelu,
                                     bias=gb[:, 1:2]).then_inc(a_f2.sem, 1)

            def phase2(b, after):
                for n in range(PAIRS + 3):
                    if n < PAIRS:
                        gelu1(b, n)
                    if 0 <= n - 2 < PAIRS:
                        gelu2(b, n - 2)
                    if after is not None and n == 8:
                        x_high(after, b)
                if after is not None:
                    for c in range(4):
                        values(after, c)

            act.wait_ge(w_small, SMALL_ALL)
            act.wait_ge(k_pool, 2)
            prepare_weights()
            x_high(0, None)
            for c in range(4):
                values(0, c)
            phase1(0)
            with act.Fori(0, BATCHES - 2) as b:
                phase2(b, b + 1)
                phase1(b + 1)
            phase2(BATCHES - 2, BATCHES - 1)
            phase1(BATCHES - 1)
            phase2(BATCHES - 1, None)

            def block_transposed(k):
                s_zt.wait(act, k, 1)
                copy(zT[:, :], bank[6][:, :], scale=normw[:, :]).then_inc(a_zt.sem, 1)

            def shares(k):
                d_st.wait(act, k, GAP)
                nc.scalar.activation(th[:, :], gap[:, :], ACT.Tanh, scale=0.5).then_inc(a_th.sem, 1)

            def experts(k, after):
                for i in range(EXPERTS * NC):
                    n = CHUNKS[i % NC][1]
                    s_gt.wait(act, k, i + 1)
                    if i >= 2:
                        d_h.wait(act, k, i - 1)
                    nc.scalar.activation(sg[0:n, i % 2, :], bank[i % 2][0:n, :], ACT.Silu).then_inc(a_sg.sem, 1)
                    if after is not None and i == 4 * NC:
                        block_transposed(after)
                    if after is not None and i == 7 * NC:
                        shares(after)

            block_transposed(0)
            shares(0)
            with act.Fori(0, BLOCKS - 1) as k:
                experts(k, k + 1)
            experts(BLOCKS - 1, None)

        @block.vector
        def _(dve):
            V = nc.vector

            def split(hi, lo, src, sign=1.0):
                return V.tensor_scalar(hi, src, sign, None, ALU.mult), lo

            def prepare_weights():
                dve.wait_ge(k_pool, 3)
                V.tensor_copy(ident_bf[:, :], ident[:, :])
                for a in range(2):
                    V.tensor_copy(mask[:, a, :], maskf[:, :])
                dve.wait_ge(w_small, SMALL_ALL)
                V.tensor_tensor(gwi[:, :], gw[:, 0, :], ident[:, :], ALU.add).then_inc(k_dve, 1)
                dve.wait_ge(w_w, 5 * 16)
                V.tensor_copy(v_hi[:, :], raw[:, 2, :])
                for n in range(2):
                    V.tensor_copy(w_hi[:, n, :], raw[:, n, :])
                V.tensor_scalar(w_hi[:, 2, :], raw[:, 2, :], -1.0, None, ALU.mult).then_inc(k_dve, 1)
                dve.wait_ge(k_dve, 2)
                V.tensor_tensor(v_lo[:, :], raw[:, 2, :], v_hi[:, :].bitcast(f32), ALU.subtract)
                for n in range(2):
                    V.tensor_tensor(w_lo[:, n, :], raw[:, n, :], w_hi[:, n, :].bitcast(f32), ALU.subtract)
                V.scalar_tensor_tensor(w_lo[:, 2, :], raw[:, 2, :], -1.0, w_hi[:, 2, :].bitcast(f32),
                                       ALU.mult, ALU.subtract).then_inc(k_dve, 1)
                dve.wait_ge(k_pe, 1)
                for h in range(2):
                    V.tensor_copy(mv_hi[:, h * 512:(h + 1) * 512], bank[h][:, :]).then_inc(k_dve, 1)
                dve.wait_ge(k_dve, 5)
                for h in range(2):
                    cols = slice(h * 512, (h + 1) * 512)
                    V.tensor_tensor(mv_lo[:, cols], bank[h][:, :], mv_hi[:, cols].bitcast(f32),
                                    ALU.subtract)
                dve.wait_ge(k_pe, 3)
                V.tensor_copy(cy_hi[:, :], bank[4][:, 0:P]).then_inc(k_dve, 1)
                dve.wait_ge(k_dve, 6)
                V.tensor_tensor(cy_lo[:, :], bank[4][:, 0:P], cy_hi[:, :].bitcast(f32),
                                ALU.subtract).then_inc(k_dve, 1)
                dve.wait_ge(k_act, 1)
                dve.wait_ge(k_dve, 7)
                V.tensor_copy(rs[:, 0, 0:1], gin[:, :]).then_inc(k_dve, 1)

            def wait_ahead(signal, turn, k):
                signal.wait(dve, turn, k)
                V.memset(hold[:, :], 0.0)

            def stats(b, src, step):
                for t in range(TILES):
                    done = V.bn_stats(stat[:, t, :], src(t))
                done.then_inc(d_ln.sem, 1)

            def aggregate(b, step):
                wait_ahead(d_ln, b, step)
                for t in range(TILES):
                    done = V.bn_aggr(mv_[:, t, :], stat[:, t, :])
                done.then_inc(d_ln.sem, 1)
                d_ln.wait(dve, b, step + 1)
                V.tensor_scalar(ve[:, :], mv_[:, :, 1], EPS_LN, None, ALU.add).then_inc(d_ln.sem, 1)

            def normalise(b, step, power, o, src):
                p_ln.wait(dve, b, power)
                for t in range(TILES):
                    done = V.tensor_scalar(o[:, t, :], src(t), mv_[:, t, 0:1], rstd[:, t:t + 1],
                                           ALU.subtract, ALU.mult)
                done.then_inc(d_ln.sem, 1)

            def x_tile(b):
                return lambda t: x_all[:, bass.ds(b * TILES + t, 1), :].rearrange("p o d -> p (o d)")

            def norm_step(b, i):
                if i == 0:
                    stats(b, x_tile(b), 0)
                if i == 1:
                    aggregate(b, 1)
                if i == 2:
                    normalise(b, 3, 1, xh, x_tile(b))
                if i == 3:
                    wait_ahead(d_ln, b, 4)
                    stats(b, lambda t: xh[:, t, :], 4)
                if i == 4:
                    aggregate(b, 5)
                if i == 5:
                    normalise(b, 7, 2, xn, lambda t: xh[:, t, :])

            def x_low(b):
                a_xt.wait(dve, b, 1)
                V.scalar_tensor_tensor(xt_lo[:, :], bank[6][:, 0:TOKENS], gin[:, :],
                                       xt_hi[:, :].bitcast(f32), ALU.mult, ALU.subtract).then_inc(d_xt.sem, 1)

            def maxima(b, n):
                for t in range(2):
                    s_s.wait(dve, b, 2 * n + 1 + t)
                    width = (t + 1) * P
                    V.tensor_reduce(nmax[:, n % 3, 2 * t:2 * t + 2],
                                    bank[1 + t][:, 0:2 * width].rearrange("p (a j) -> p a j", a=2), X, ALU.max,
                                    negate=True).then_inc(d_max.sem, 1)

            def adjacency(b, n):
                s = n % 3
                a_exp.wait(dve, b, 2 * n + 2)
                V.reciprocal(rs[:, s, :], ssum[:, s, :])
                for a in range(2):
                    V.scalar_tensor_tensor(ea[:, s, a, :], ident[:, :], ssum[:, s, a:a + 1], ea[:, s, a, :],
                                           ALU.mult, ALU.max, accum_out=den[:, s, a:a + 1])
                for a in range(2):
                    done = V.scalar_tensor_tensor(eb[:, s, a, :], idw[:, :], ssum[:, s, 2 + a:3 + a],
                                                  eb[:, s, a, :], ALU.mult, ALU.max,
                                                  accum_out=den[:, s, 2 + a:3 + a])
                done.then_inc(d_e.sem, 1)
                d_e.wait(dve, b, n + 1)
                V.reciprocal(wgt[:, s, :], den[:, s, :]).then_inc(d_w.sem, 1)

            def attended(b, n):
                s_deg.wait(dve, b, n + 1)
                a_d.wait(dve, b, n + 1)
                V.tensor_tensor(aT[:, n, :], bank[6][:, 0:TOKENS], dT[:, n, :], ALU.mult).then_inc(d_a.sem, 1)

            def output_bias(b):
                s_y.wait(dve, b, 1)
                V.tensor_scalar(yT[:, :], bank[7][:, 0:TOKENS], yb[:, :], None, ALU.add).then_inc(d_yT.sem, 1)

            def output_kept(b):
                s_yn.wait(dve, b, 1)
                V.tensor_copy(y_all[:, tokens(b), :],
                              bank[7][:, 0:TOKENS].rearrange("p (t d) -> p t d", t=TILES)).then_inc(d_y.sem, 1)

            def phase1(b, before):
                if before is not None:
                    output_bias(before)
                for n in range(PAIRS + 3):
                    if n < PAIRS:
                        maxima(b, n)
                    if 0 <= n - 1 < PAIRS:
                        adjacency(b, n - 1)
                    if 0 <= n - 3 < PAIRS:
                        attended(b, n - 3)
                    if n == 2 and before is not None:
                        output_kept(before)

            def layer2_in(b, n):
                s_g1.wait(dve, b, n + 1)
                V.tensor_copy(g1[:, n % 2, :, :],
                              bank[2 + n % 2][:, 0:TOKENS].rearrange("p (t d) -> p t d", t=TILES)).then_inc(d_g1.sem, 1)

            def layer2_out(b, n):
                s_h2.wait(dve, b, n + 1)
                V.tensor_tensor(z2[:, n % 2, :], bank[4 + n % 2][:, 0:TOKENS], f1T[:, n % 4, :],
                                ALU.add).then_inc(d_z2.sem, 1)

            def phase2(b, after):
                for n in range(PAIRS + 2):
                    if 0 <= n - 1 < PAIRS:
                        layer2_in(b, n - 1)
                    if 0 <= n - 2 < PAIRS:
                        layer2_out(b, n - 2)
                    if after is not None:
                        norm_step(after, n)
                        if n == 9:
                            x_low(after)

            dve.wait_ge(w_x0, 16)
            for i in range(6):
                norm_step(0, i)
            prepare_weights()
            x_low(0)
            phase1(0, None)
            dve.wait_ge(w_x, 16)
            with dve.Fori(0, BATCHES - 2) as b:
                phase2(b, b + 1)
                phase1(b + 1, b)
            phase2(BATCHES - 2, BATCHES - 1)
            phase1(BATCHES - 1, BATCHES - 2)
            phase2(BATCHES - 1, None)
            output_bias(BATCHES - 1)
            output_kept(BATCHES - 1)

            def split_gate_up(e):
                dve.wait_ge(w_gu[e % 2], 16 * (e // 2 + 1))
                V.tensor_copy(gu_hi[:, e, :], raw_gu[:, e % 2, :]).then_inc(k_gu, 1)
                dve.wait_ge(k_gu, 2 * e + 1)
                V.tensor_tensor(gu_lo[:, e, :], raw_gu[:, e % 2, :], gu_hi[:, e, :].bitcast(f32),
                                ALU.subtract).then_inc(k_gu, 1)

            class Steps:

                def __init__(self, k, n):
                    self.k, self.n = k, n

                def done(self, ins):
                    self.n += 1
                    ins.then_inc(d_st.sem, 1)

                def ready(self):
                    d_st.wait(dve, self.k, self.n)

                def ready_ahead(self):
                    wait_ahead(d_st, self.k, self.n)

            def norms(k):
                s = Steps(k, 0)
                now = bass.ds(k * BT, BT)
                y, x1 = y_all[:, now, :], x_all[:, now, :]

                def tile(whole, t):
                    return whole[:, bass.ds(k * BT + t, 1), :].rearrange("p o d -> p (o d)")

                def moments(src):
                    if s.n:
                        s.ready_ahead()
                    for t in range(BT):
                        last = V.bn_stats(st4[:, t, :], src(t))
                    s.done(last)
                    s.ready_ahead()
                    for t in range(BT):
                        last = V.bn_aggr(mv4[:, t, :], st4[:, t, :])
                    s.done(last)
                    s.ready()
                    s.done(V.tensor_scalar(ve4[:, :], mv4[:, :, 1], EPS_LN, None, ALU.add))

                moments(lambda t: tile(y_all, t))
                p_st.wait(dve, k, 1)
                for t in range(BT):
                    last = V.tensor_scalar(t4[:, t, :], tile(y_all, t), mv4[:, t, 0:1], rs4[:, t:t + 1],
                                           ALU.subtract, ALU.mult)
                s.done(last)
                s.ready()
                s.done(V.tensor_tensor(t4[:, :, :], t4[:, :, :],
                                       gout[:, :].unsqueeze(1).to_broadcast([P, BT, DIM]), ALU.mult))
                s.ready()
                s.done(V.tensor_tensor(x1, x1, t4[:, :, :], ALU.add))
                moments(lambda t: tile(x_all, t))
                p_st.wait(dve, k, 2)
                for t in range(BT):
                    last = V.tensor_scalar(t4[:, t, :], tile(x_all, t), mv4[:, t, 0:1], rs4[:, t:t + 1],
                                           ALU.subtract, ALU.mult)
                s.done(last)
                s.ready()
                s.done(V.tensor_tensor(x1, x1, t4[:, :, :], ALU.add))
                for t in range(BT):
                    last = V.scalar_tensor_tensor(sq4[:, t, :], t4[:, t, :], 1.0, t4[:, t, :], ALU.mult,
                                                  ALU.mult, accum_out=ss4[:, t:t + 1])
                s.done(last)
                s.ready()
                s.done(V.tensor_scalar(ve4[:, :], ss4[:, :], 1.0 / DIM, EPS_RMS, ALU.mult, ALU.add))
                p_st.wait(dve, k, 3)
                for t in range(BT):
                    last = V.tensor_scalar(z4[:, t, :], t4[:, t, :], rs4[:, t:t + 1], None, ALU.mult)
                s.done(last)
                assert s.n == NORMED

            def z_split(k):
                s = Steps(k, NORMED)
                a_zt.wait(dve, k, 1)
                s.ready()
                s.done(V.tensor_copy(zt_hi[:, bass.ds(k * BLOCK, BLOCK)], zT[:, :]))
                s.ready()
                V.tensor_tensor(zt_lo[:, bass.ds(k * BLOCK, BLOCK)], zT[:, :],
                                zt_hi[:, bass.ds(k * BLOCK, BLOCK)].bitcast(f32), ALU.subtract).then_inc(d_zl.sem, 1)
                assert s.n == SPLIT

            def best_two(k):
                s = Steps(k, SPLIT)
                s_lg.wait(dve, k, 1)
                s.done(V.tensor_copy(lg[:, :, :], bank[7][:, 0:BT * EXPERTS].rearrange("p (t e) -> p t e", t=BT)))
                s.ready_ahead()
                for t in range(BT):
                    last = V.max(top[:, t, :], lg[:, t, :])
                s.done(last)
                s.ready()
                s.done(V.tensor_tensor(gap[:, :], top[:, :, 0], top[:, :, 1], ALU.subtract))
                for t in range(BT):
                    last = V.max_index(topi[:, t, :], top[:, t, :], lg[:, t, :])
                s.done(last)
                s.ready()
                s.done(V.tensor_copy(topf[:, :, :], topi[:, :, 0:2]))
                s.ready()
                dve.wait_ge(k_pool, 4)
                for r in range(2):
                    last = V.tensor_tensor(eq[:, r, :, :], iot[:, :].unsqueeze(1).to_broadcast([P, BT, EXPERTS]),
                                           topf[:, :, r:r + 1].to_broadcast([P, BT, EXPERTS]), ALU.is_equal)
                s.done(last)
                assert s.n == CHOSEN

            def shares(k):
                s = Steps(k, CHOSEN)
                a_th.wait(dve, k, 1)
                V.tensor_scalar(wt2[:, 0, :], th[:, :], 1.0, 0.5, ALU.add, ALU.mult)
                s.done(V.tensor_scalar(wt2[:, 1, :], th[:, :], -0.5, 0.5, ALU.mult, ALU.add))
                s.ready()
                s.done(V.tensor_scalar(wt2[:, :, :], wt2[:, :, :], alph[:, :], None, ALU.mult))
                s.ready()
                for r in range(2):
                    last = V.tensor_tensor(eq[:, r, :, :], eq[:, r, :, :],
                                           wt2[:, r, :].unsqueeze(2).to_broadcast([P, BT, EXPERTS]), ALU.mult)
                s.done(last)
                s.ready()
                V.tensor_tensor(comb[:, bass.ds(k, 1), :, :].rearrange("p o t e -> p (o t) e"), eq[:, 0, :, :],
                                eq[:, 1, :, :], ALU.add).then_inc(d_comb.sem, 1)
                assert s.n == d_st.per == ROUTED

            def hidden(k, i):
                e, c = i // NC, i % NC
                n = CHUNKS[c][1]
                a_sg.wait(dve, k, i + 1)
                s_up.wait(dve, k, i + 1)
                if c == 0 and e >= 2:
                    s_dn.wait(dve, k, e - 1)
                V.tensor_tensor(hT[0:n, e % 2, c, :], bank[2 + i % 2][0:n, :], sg[0:n, i % 2, :],
                                ALU.mult).then_inc(d_h.sem, 1)

            def add_expert(k, slot, e):
                s_dn.wait(dve, k, e + 1)
                if e > 0:
                    d_acc.wait(dve, k, e)
                for t in range(BT):
                    into = acc[:, slot, t, :]
                    w = comb[:, bass.ds(k, 1), t, e:e + 1].rearrange("p o e -> p (o e)")
                    src = x_all[:, bass.ds(k * BT + t, 1), :].rearrange("p o d -> p (o d)") if e == 0 else into
                    last = V.scalar_tensor_tensor(into, bank[4 + e % 2][:, xt(t)], w, src, ALU.mult, ALU.add)
                last.then_inc(d_acc.sem, 1)

            def experts(k, slot, after, loading=False, turn=None):
                d_comb.wait(dve, k, 1)
                if turn is not None:
                    o_out[slot].wait(dve, turn, 0)
                for e in range(EXPERTS):
                    if loading and e + 1 < EXPERTS:
                        split_gate_up(e + 1)
                    for c in range(NC):
                        hidden(k, e * NC + c)
                        if c == 1 and e > 0:
                            add_expert(k, slot, e - 1)
                    if after is not None:
                        if e == 1:
                            norms(after)
                        if e == 5:
                            z_split(after)
                        if e == 6:
                            best_two(after)
                        if e == 7:
                            shares(after)
                add_expert(k, slot, EXPERTS - 1)

            V.tensor_scalar(alph[:, :], alph[:, :], -0.5, 2.0, ALU.max, ALU.min).then_inc(k_dve, 1)
            dve.wait_ge(k_dve, 9)
            norms(0)
            z_split(0)
            split_gate_up(0)
            best_two(0)
            shares(0)
            experts(0, 0, 1, loading=True)
            experts(1, 1, 2)
            with dve.Fori(1, BLOCKS // 2 - 1) as i:
                experts(i * 2, 0, i * 2 + 1, turn=i)
                experts(i * 2 + 1, 1, i * 2 + 2, turn=i)
            experts(BLOCKS - 2, 0, BLOCKS - 1, turn=BLOCKS // 2 - 1)
            experts(BLOCKS - 1, 1, None, turn=BLOCKS // 2 - 1)


def kernel(**inputs):
    import numpy as np
    import concourse.bacc as bacc
    from concourse.bass_utils import run_bass_kernel_spmd

    a = {n[3:]: np.asarray(v) for n, v in inputs.items()}
    given = dict(
        x=a["attn_x"].reshape(ALL, DIM), wq=a["attn_Wq"], wk=a["attn_Wk"], wv=a["attn_Wv"],
        wvT=a["attn_Wv"].T, gnn_w=a["attn_gnn_w"], gnn_b=a["attn_gnn_b"], lin_wT=a["attn_lin_w"].T,
        lin_b=a["attn_lin_b"].reshape(DHEAD, 1), wo=a["attn_Wo"], gamma_in=a["attn_gamma_in"].reshape(DIM, 1),
        gamma_out=a["attn_gamma_out"].reshape(1, DIM), norm_w=a["ffn_norm_weight"].reshape(DIM, 1),
        routerT=a["ffn_router_weight"].T, guT=a["ffn_gate_up_weight"].transpose(0, 2, 1),
        downT=a["ffn_down_weight"].transpose(0, 2, 1), alpha=a["ffn_residual_alpha"].reshape(1, 1))
    given = {n: np.ascontiguousarray(v) for n, v in given.items()}
    nc = bacc.Bacc("TRN2", target_bir_lowering=False, num_devices=1)
    args = {n: nc.dram_tensor(f"in_{n}", v.shape, f32, kind="ExternalInput").ap() for n, v in given.items()}
    out = nc.dram_tensor("out", (ALL, DIM), f32, kind="ExternalOutput").ap()
    build_program(nc, out=out, **args)
    r = run_bass_kernel_spmd(nc, [{f"in_{n}": v for n, v in given.items()}], core_ids=[0])
    return r.results[0]["out"].reshape(BATCHES, TOKENS, DIM)
```

```python
from contextlib import ExitStack

import concourse.bass as bass
from concourse import mybir

P = 128
BATCHES, TOKENS, DIM = 16, 256, 128
HEADS, DHEAD = 16, 64
PAIRS = HEADS // 2
TILES = TOKENS // P
HD = HEADS * DHEAD
ALL = BATCHES * TOKENS
EXPERTS, HID = 8, 352
BLOCK = 512
BLOCKS, BT = ALL // BLOCK, BLOCK // P
CHUNKS = [(c, min(P, HID - c)) for c in range(0, HID, P)]
NC = len(CHUNKS)
EPS_LN, EPS_RMS = 1e-5, 1e-6
MASKED = -3.0e38
SCALE = DHEAD ** -0.5

f32, f32r, bf16, u32 = mybir.dt.float32, mybir.dt.float32r, mybir.dt.bfloat16, mybir.dt.uint32
ALU = mybir.AluOpType
ACT = mybir.ActivationFunctionType
X = mybir.AxisListType.X


class Signal:

    def __init__(self, sem, per):
        self.sem, self.per = sem, per

    def wait(self, engine, turn, k):
        engine.wait_ge(self.sem, turn * self.per + k)


def build_program(nc, x, wq, wk, wv, wvT, gnn_w, gnn_b, lin_wT, lin_b, wo, gamma_in, gamma_out,
                  norm_w, routerT, guT, downT, alpha, out):
    ctx = ExitStack()
    attn = ExitStack()

    def sb(name, shape, dt=f32, where=ctx):
        return where.enter_context(nc.sbuf_tensor(name, shape, dt))

    def sem(name):
        return ctx.enter_context(nc.semaphore(name))

    with ctx:
        bank = [ctx.enter_context(nc.psum_tensor(f"bank{i}", [P, 512], f32)) for i in range(8)]

        x_all = sb("x_all", [P, BATCHES * TILES, DIM])
        y_all = sb("y_all", [P, BATCHES * TILES, DIM])
        ident = sb("ident", [P, P])
        half = sb("half", [P, BT])
        gout = sb("gout", [P, DIM])
        normw = sb("normw", [P, 1])
        hold = sb("hold", [P, 1])
        rtT = sb("rtT", [P, EXPERTS])
        alph = sb("alph", [P, 1])

        lb = sb("lb", [P, 1])
        gin = sb("gin", [P, 1])
        yb = sb("yb", [P, 1])
        yT = sb("yT", [P, TOKENS])
        zT = sb("zT", [P, BLOCK])
        st4 = sb("st4", [P, BT, 6])
        mv4 = sb("mv4", [P, BT, 2])
        ve4 = sb("ve4", [P, BT])
        rs4 = sb("rs4", [P, BT])
        t4 = sb("t4", [P, BT, DIM])
        z4 = sb("z4", [P, BT, DIM])
        sq4 = sb("sq4", [P, BT, DIM])
        ss4 = sb("ss4", [P, BT])
        lg = sb("lg", [P, BT, EXPERTS])
        top = sb("top", [P, BT, 8])
        topi = sb("topi", [P, BT, 8], u32)
        topf = sb("topf", [P, BT, 2])
        iot = sb("iot", [P, EXPERTS])
        gap = sb("gap", [P, BT])
        th = sb("th", [P, BT])
        wt2 = sb("wt2", [P, 2, BT])
        eq = sb("eq", [P, 2, BT, EXPERTS])
        comb = sb("comb", [P, BLOCKS, BT, EXPERTS])

        def at(name, shape, dt=f32):
            return sb(name, shape, dt, attn)

        raw = at("raw", [P, 3, HD])
        wvt = at("wvt", [P, PAIRS, P])
        gwi = at("gwi", [P, P])
        linT = at("linT", [P, P])
        maskf = at("maskf", [P, P])
        w_hi = at("w_hi", [P, 3, HD], f32r)
        w_lo = at("w_lo", [P, 3, HD], f32r)
        v_hi = at("v_hi", [P, HD], f32r)
        v_lo = at("v_lo", [P, HD], f32r)
        vnat = at("vnat", [P, TILES, HD])
        ea = at("ea", [P, 3, 2, P])
        eb = at("eb", [P, 3, 2, 2 * P])
        deg = at("deg", [P, 3, 4, DHEAD])
        qT = at("qT", [P, 2, TOKENS])
        kT = at("kT", [P, 2, 2, TOKENS])
        gt0 = at("gt0", [P, PAIRS, 2, TOKENS])
        gt1 = at("gt1", [P, PAIRS, 2, P])
        dT = at("dT", [P, PAIRS, TOKENS])
        aT = at("aT", [P, PAIRS, TOKENS])
        f1T = at("f1T", [P, 4, TOKENS])
        g1 = at("g1", [P, 2, TILES, P])
        z2 = at("z2", [P, 2, TOKENS])
        f2T = at("f2T", [P, 2, TOKENS])
        wo_sb = at("wo_sb", [P, PAIRS, P])
        gw = at("gw", [P, 2, P])
        gb = at("gb", [P, 2])
        mv_hi = at("mv_hi", [P, HD], f32r)
        mv_lo = at("mv_lo", [P, HD], f32r)
        cy_hi = at("cy_hi", [P, P], f32r)
        cy_lo = at("cy_lo", [P, P], f32r)
        lwo = at("lwo", [P, PAIRS, P])
        ident_bf = at("ident_bf", [P, P], bf16)
        mask = at("mask", [P, 2, P], bf16)
        idw = at("idw", [P, 2 * P])
        stat = at("stat", [P, TILES, 6])
        mv_ = at("mv_", [P, TILES, 2])
        ve = at("ve", [P, TILES])
        rstd = at("rstd", [P, TILES])
        xh = at("xh", [P, TILES, DIM])
        xn = at("xn", [P, TILES, DIM])
        xt_hi = at("xt_hi", [P, TOKENS], f32r)
        xt_lo = at("xt_lo", [P, TOKENS], f32r)
        nmax = at("nmax", [P, 3, 4])
        ssum = at("ssum", [P, 3, 4])
        den = at("den", [P, 3, 4])
        rs = at("rs", [P, 3, 4])
        wgt = at("wgt", [P, 3, 4])
        attn.close()

        raw_gu = sb("raw_gu", [P, 2, 2 * HID])
        dn = sb("dn", [P, EXPERTS, NC, DIM])
        gu_hi = sb("gu_hi", [P, EXPERTS, 2 * HID], f32r)
        gu_lo = sb("gu_lo", [P, EXPERTS, 2 * HID], f32r)
        zt = sb("zt", [P, BLOCKS, 2, BLOCK], f32r)
        hT = sb("hT", [P, 2, NC, BLOCK])
        sg = sb("sg", [P, 2, BLOCK])
        acc = sb("acc", [P, 2, BT, DIM])

        w_x0, w_x, w_w, w_small = sem("w_x0"), sem("w_x"), sem("w_w"), sem("w_small")
        w_gu = [sem(f"w_gu{i}") for i in range(2)]
        w_dn = sem("w_dn")
        k_pool, k_dve, k_pe, k_act = sem("k_pool"), sem("k_dve"), sem("k_pe"), sem("k_act")
        d_ln = Signal(sem("d_ln"), 8)
        p_ln = Signal(sem("p_ln"), 2)
        s_xt = Signal(sem("s_xt"), 1)
        a_xt = Signal(sem("a_xt"), 1)
        d_xt = Signal(sem("d_xt"), 1)
        s_v = Signal(sem("s_v"), 4)
        a_v = Signal(sem("a_v"), 4)
        s_qk, a_qk = Signal(sem("s_qk"), PAIRS), Signal(sem("a_qk"), PAIRS)
        s_s = Signal(sem("s_s"), 2 * PAIRS)
        d_max = Signal(sem("d_max"), 2 * PAIRS)
        a_exp = Signal(sem("a_exp"), 2 * PAIRS)
        d_e = Signal(sem("d_e"), PAIRS)
        d_w = Signal(sem("d_w"), PAIRS)
        p_deg = Signal(sem("p_deg"), PAIRS)
        p_g = Signal(sem("p_g"), PAIRS)
        s_t, a_gt = Signal(sem("s_t"), PAIRS), Signal(sem("a_gt"), PAIRS)
        s_d, a_d = Signal(sem("s_d"), PAIRS), Signal(sem("a_d"), PAIRS)
        s_deg = Signal(sem("s_deg"), PAIRS)
        d_a = Signal(sem("d_a"), PAIRS)
        s_f1, a_f1 = Signal(sem("s_f1"), PAIRS), Signal(sem("a_f1"), PAIRS)
        s_g1, d_g1 = Signal(sem("s_g1"), PAIRS), Signal(sem("d_g1"), PAIRS)
        s_h2, d_z2 = Signal(sem("s_h2"), PAIRS), Signal(sem("d_z2"), PAIRS)
        a_f2 = Signal(sem("a_f2"), PAIRS)
        s_y, d_yT = Signal(sem("s_y"), 1), Signal(sem("d_yT"), 1)
        s_yn, d_y = Signal(sem("s_yn"), 1), Signal(sem("d_y"), 1)
        d_st = Signal(sem("d_st"), 24)
        p_st = Signal(sem("p_st"), 3)
        s_zt, a_zt, d_zl = Signal(sem("s_zt"), 1), Signal(sem("a_zt"), 1), Signal(sem("d_zl"), 1)
        s_lg, a_th, d_comb = Signal(sem("s_lg"), 1), Signal(sem("a_th"), 1), Signal(sem("d_comb"), 1)
        k_gu = sem("k_gu")
        s_gt = Signal(sem("s_gt"), EXPERTS * NC)
        s_up = Signal(sem("s_up"), EXPERTS * NC)
        a_sg = Signal(sem("a_sg"), EXPERTS * NC)
        d_h = Signal(sem("d_h"), EXPERTS * NC)
        s_dn = Signal(sem("s_dn"), EXPERTS)
        d_acc = Signal(sem("d_acc"), EXPERTS)
        o_out = [Signal(sem(f"o_out{i}"), 16) for i in range(2)]

        def xt(t):
            return slice(t * P, (t + 1) * P)

        def tokens(b):
            return bass.ds(b * TILES, TILES)

        block = ctx.enter_context(nc.Block())

        @block.sync
        def _(sp):
            xv = x.rearrange("(t p) d -> p t d", p=P)
            sp.dma_start(x_all[:, 0:TILES, :], xv[:, 0:TILES, :]).then_inc(w_x0, 16)
            for dst, src in ((gin[:, :], gamma_in), (normw[:, :], norm_w), (rtT[:, :], routerT),
                             (gout[:, :], gamma_out.to_broadcast([P, DIM])),
                             (alph[:, :], alpha.to_broadcast([P, 1]))):
                sp.dma_start(dst, src).then_inc(w_small, 16)
            for n, w in enumerate((wq, wk, wv)):
                sp.dma_start(raw[:, n, :], w).then_inc(w_w, 16)
            sp.dma_start(wvt[:, :, :], wvT.rearrange("(g p) d -> p g d", p=P)).then_inc(w_w, 16)
            sp.dma_start(wo_sb[:, :, :], wo.rearrange("(g p) d -> p g d", p=P)).then_inc(w_w, 16)
            sp.wait_ge(k_pool, 1)
            for h in range(2):
                at_ = slice(h * DHEAD, (h + 1) * DHEAD)
                for l in range(2):
                    sp.dma_start(gw[at_, l, at_], gnn_w[l]).then_inc(w_small, 16)
                    sp.dma_start(gb[at_, l:l + 1], gnn_b[l:l + 1, :].rearrange("o d -> d o")).then_inc(w_small, 16)
                sp.dma_start(linT[at_, at_], lin_wT).then_inc(w_small, 16)
                sp.dma_start(lb[at_, :], lin_b).then_inc(w_small, 16)
            sp.dma_start(x_all[:, TILES:, :], xv[:, TILES:, :]).then_inc(w_x, 16)

            sp.wait_ge(k_dve, 8)
            for c, (at_, n) in enumerate(CHUNKS):
                sp.dma_start(dn[0:n, :, c, :], downT[:, at_:at_ + n, :].rearrange("e p d -> p e d")).then_inc(w_dn, 16)
            for e in range(EXPERTS):
                if e >= 2:
                    sp.wait_ge(k_gu, 2 * (e - 1))
                sp.dma_start(raw_gu[:, e % 2, :], guT[e]).then_inc(w_gu[e % 2], 16)
            ov = out.rearrange("(k t p) d -> k p t d", p=P, t=BT)
            with sp.Fori(0, BLOCKS // 2) as i:
                for half_ in range(2):
                    k = i * 2 + half_
                    d_acc.wait(sp, k, EXPERTS)
                    sp.dma_start(ov[bass.ds(k, 1), :, :, :].rearrange("o p t d -> p (o t) d"),
                                 acc[:, half_, :, :]).then_inc(o_out[half_].sem, 16)
            for done in o_out:
                done.wait(sp, BLOCKS // 2, 0)

        SMALL_ALL = 17 * 16
        POWERS = (3, 9, 13)
        NORMED, SPLIT, GAP, CHOSEN, ROUTED = 14, 15, 18, 21, 24

        @block.gpsimd
        def _(pool):
            nc.gpsimd.memset(gw[:, :, :], 0.0)
            nc.gpsimd.memset(linT[:, :], 0.0).then_inc(k_pool, 1)
            nc.gpsimd.memset(half[:, :], -0.5)
            nc.gpsimd.memset(ident[:, :], 0.0)
            nc.gpsimd.memset(idw[:, :], 0.0)
            nc.gpsimd.memset(maskf[:, :], 0.0)
            nc.gpsimd.memset(kT[:, :, :, :], 0.0).then_inc(k_pool, 1)
            pool.wait_ge(k_pool, 2)
            for m in (ident[:, :], idw[:, P:2 * P]):
                nc.gpsimd.affine_select(out=m, in_=m, compare_op=ALU.not_equal, fill=1.0,
                                        base=0, pattern=[[-1, P]], channel_multiplier=1)
            nc.gpsimd.affine_select(out=maskf[:, :], in_=maskf[:, :], compare_op=ALU.is_ge, fill=MASKED,
                                    base=0, pattern=[[-1, P]], channel_multiplier=1)
            nc.gpsimd.iota(iot[:, :], pattern=[[1, EXPERTS]], base=0, channel_multiplier=0,
                           allow_small_or_imprecise_dtypes=True).then_inc(k_pool, 1)

            def deviation(b, step, d_step):
                d_ln.wait(pool, b, d_step)
                nc.gpsimd.tensor_tensor(rstd[:, :], ve[:, :], half[:, 0:TILES], ALU.pow).then_inc(p_ln.sem, 1)

            def graph(b, n):
                s = n % 3
                d_w.wait(pool, b, n + 1)
                nc.gpsimd.tensor_tensor(ea[:, s], ea[:, s],
                                        wgt[:, s, 0:2].unsqueeze(2).to_broadcast([P, 2, P]), ALU.mult)
                nc.gpsimd.tensor_tensor(eb[:, s], eb[:, s],
                                        wgt[:, s, 2:4].unsqueeze(2).to_broadcast([P, 2, 2 * P]),
                                        ALU.mult).then_inc(p_g.sem, 1)
                nc.gpsimd.tensor_tensor(deg[:, s], den[:, s, :].unsqueeze(2).to_broadcast([P, 4, DHEAD]),
                                        rs[:, s, :].unsqueeze(2).to_broadcast([P, 4, DHEAD]),
                                        ALU.mult).then_inc(p_deg.sem, 1)

            deviation(0, 0, 3)
            deviation(0, 1, 7)
            for n in range(PAIRS):
                graph(0, n)
            with pool.Fori(0, BATCHES - 1) as b:
                deviation(b + 1, 0, 3)
                deviation(b + 1, 1, 7)
                for n in range(PAIRS):
                    graph(b + 1, n)

            def prepare(k):
                for i, step in enumerate(POWERS):
                    d_st.wait(pool, k, step)
                    nc.gpsimd.tensor_tensor(rs4[:, :], ve4[:, :], half[:, :], ALU.pow).then_inc(p_st.sem, 1)

            prepare(0)
            with pool.Fori(0, BLOCKS - 1) as k:
                prepare(k + 1)

        @block.tensor
        def _(pe):
            def product(o, st, mo, first, last, **more):
                nc_mm = nc.tensor.matmul
                return nc_mm(o, st, mo, start=first, stop=last, **more)

            def product3(o, st_hi, st_lo, mo_hi, mo_lo, first=True, last=True, **more):
                product(o, st_hi, mo_lo, first, False, **more)
                product(o, st_lo, mo_hi, False, False, **more)
                return product(o, st_hi, mo_hi, False, last, **more)

            def prepare_weights():
                pe.wait_ge(k_pool, 3)
                pe.wait_ge(w_w, 5 * 16)
                pe.wait_ge(w_small, SMALL_ALL)
                pe.wait_ge(k_dve, 1)
                for g in range(PAIRS):
                    mm = product(bank[g // 4][:, (g % 4) * P:(g % 4 + 1) * P], wvt[:, g, :], gwi[:, :], True, True)
                mm.then_inc(k_pe, 1)
                for g in range(PAIRS):
                    mm = product(bank[2 + g // 4][:, (g % 4) * P:(g % 4 + 1) * P], linT[:, :], wo_sb[:, g, :], True, True)
                mm.then_inc(k_pe, 1)
                for g in range(PAIRS):
                    mm = product(bank[4][:, 0:P], wvt[:, g, :], wo_sb[:, g, :], g == 0, g == PAIRS - 1)
                for g in range(PAIRS):
                    mm = product(bank[5][:, 0:1], wo_sb[:, g, :], lb[:, :], g == 0, g == PAIRS - 1)
                mm.then_inc(k_pe, 1)

            def x_transposed(b):
                d_ln.wait(pe, b, 8)
                for t in range(TILES):
                    mm = nc.tensor.transpose(bank[6][:, xt(t)], xn[:, t, :], ident[:, :])
                mm.then_inc(s_xt.sem, 1)

            def values(b, c):
                t, h = c // 2, c % 2
                if c == 0:
                    a_xt.wait(pe, b, 1)
                    d_xt.wait(pe, b, 1)
                if c >= 2:
                    a_v.wait(pe, b, c - 1)
                cols = slice(h * 512, (h + 1) * 512)
                product3(bank[c % 2][:, :], xt_hi[:, xt(t)], xt_lo[:, xt(t)],
                         v_hi[:, cols], v_lo[:, cols]).then_inc(s_v.sem, 1)

            def queries_keys(b, n):
                if n == 0:
                    a_v.wait(pe, b, 3)
                else:
                    a_qk.wait(pe, b, n)
                cols = slice(n * P, (n + 1) * P)
                product3(bank[0][:, 0:TOKENS], w_hi[:, 0, cols], w_lo[:, 0, cols], xt_hi[:, :], xt_lo[:, :])
                product3(bank[0][:, TOKENS:], w_hi[:, 1, cols], w_lo[:, 1, cols],
                         xt_hi[:, :], xt_lo[:, :]).then_inc(s_qk.sem, 1)

            def scores(b, n):
                a_qk.wait(pe, b, n + 1)
                if n == 0:
                    a_v.wait(pe, b, 4)
                else:
                    a_exp.wait(pe, b, 2 * n - 1)
                q, k = qT[:, n % 2], kT[:, n % 2]
                product(bank[1][:, 0:2 * P], ident_bf[:, :], mask[:, :, :], True, False)
                product(bank[1][:, 0:2 * P], q[:, xt(0)], k[:, :, xt(0)], False, True).then_inc(s_s.sem, 1)
                if n >= 1:
                    a_exp.wait(pe, b, 2 * n)
                sb1 = bank[2][:, :].rearrange("p (h j) -> p h j", h=2)
                product(sb1[:, :, xt(1)], ident_bf[:, :], mask[:, :, :], True, False, skip_group_check=True)
                product(bank[2][:, :], q[:, xt(1)], k[:, :, :], False, True,
                        skip_group_check=True).then_inc(s_s.sem, 1)

            def transposes(b, n):
                s = n % 3
                p_g.wait(pe, b, n + 1)
                if n >= 1:
                    a_gt.wait(pe, b, n)
                for a in range(2):
                    nc.tensor.transpose(bank[3][:, a * TOKENS:a * TOKENS + P], ea[:, s, a, :], ident[:, :])
                    nc.tensor.transpose(bank[3][:, a * TOKENS + P:(a + 1) * TOKENS], eb[:, s, a, 0:P], ident[:, :])
                for a in range(2):
                    mm = nc.tensor.transpose(bank[4][:, a * P:(a + 1) * P], eb[:, s, a, P:], ident[:, :])
                mm.then_inc(s_t.sem, 1)

            def mixed(o, left, n):
                for tile, moving, cols in ((0, gt0, slice(0, TOKENS)), (1, gt1, slice(P, TOKENS))):
                    for a in range(2):
                        rows = slice(a * DHEAD, (a + 1) * DHEAD)
                        mm = product(o[rows, cols], left(tile, a), moving[:, n, a, :], tile == 0,
                                     tile == 1, skip_group_check=True)
                return mm

            def differences(b, n):
                a_gt.wait(pe, b, n + 1)
                if n == 0:
                    a_v.wait(pe, b, 4)
                else:
                    a_d.wait(pe, b, n)
                o = bank[5][:, 0:TOKENS]
                mixed(o, lambda t, a: vnat[:, t, n * P + a * DHEAD:n * P + (a + 1) * DHEAD], n)
                cols = slice(n * P, (n + 1) * P)
                product3(o, w_hi[:, 2, cols], w_lo[:, 2, cols], xt_hi[:, :], xt_lo[:, :], first=False,
                         skip_group_check=True).then_inc(s_d.sem, 1)

            def degrees(b, n):
                p_deg.wait(pe, b, n + 1)
                if n >= 1:
                    d_a.wait(pe, b, n)
                for t in range(TILES):
                    mm = nc.tensor.transpose(
                        bank[6][:, xt(t)],
                        deg[:, n % 3, 2 * t:2 * t + 2, :].rearrange("p a c -> p (a c)"), ident[:, :])
                mm.then_inc(s_deg.sem, 1)

            def output_natural(b):
                d_yT.wait(pe, b, 1)
                for t in range(TILES):
                    mm = nc.tensor.transpose(bank[7][:, xt(t)], yT[:, xt(t)], ident[:, :])
                mm.then_inc(s_yn.sem, 1)

            def layer1(b, n):
                a_d.wait(pe, b, n + 1)
                if n >= 2:
                    a_f1.wait(pe, b, n - 1)
                o = bank[n % 2][:, 0:TOKENS]
                product(o, gw[:, 0, :], dT[:, n, :], True, False)
                cols = slice(n * P, (n + 1) * P)
                product3(o, mv_hi[:, cols], mv_lo[:, cols], xt_hi[:, :], xt_lo[:, :],
                         first=False).then_inc(s_f1.sem, 1)

            def layer2_in(b, n):
                a_f1.wait(pe, b, n + 1)
                if n >= 2:
                    d_g1.wait(pe, b, n - 1)
                for t in range(TILES):
                    mm = product(bank[2 + n % 2][:, xt(t)], f1T[:, n % 4, xt(t)], gw[:, 1, :], True, True)
                mm.then_inc(s_g1.sem, 1)

            def layer2(b, n):
                d_g1.wait(pe, b, n + 1)
                if n >= 2:
                    d_z2.wait(pe, b, n - 1)
                mixed(bank[4 + n % 2][:, 0:TOKENS],
                      lambda t, a: g1[:, n % 2, t, a * DHEAD:(a + 1) * DHEAD], n).then_inc(s_h2.sem, 1)

            def output_start(b, before):
                if before is not None:
                    d_y.wait(pe, before, 1)
                product3(bank[7][:, 0:TOKENS], cy_hi[:, :], cy_lo[:, :], xt_hi[:, :], xt_lo[:, :], last=False)

            def output_graph(b, n):
                a_f2.wait(pe, b, n + 1)
                product(bank[7][:, 0:TOKENS], lwo[:, n, :], f2T[:, n % 2, :], False, False)

            def output_attended(b, pairs):
                if pairs[0] == 0:
                    d_a.wait(pe, b, PAIRS)
                for n in pairs:
                    mm = product(bank[7][:, 0:TOKENS], wo_sb[:, n, :], aT[:, n, :], False, n == PAIRS - 1)
                if n == PAIRS - 1:
                    mm.then_inc(s_y.sem, 1)

            HALVES = (range(0, PAIRS // 2), range(PAIRS // 2, PAIRS))

            def phase1(b, before):
                for n in range(PAIRS + 2):
                    if n >= 2:
                        transposes(b, n - 2)
                    if n + 1 < PAIRS:
                        queries_keys(b, n + 1)
                    if n < PAIRS:
                        scores(b, n)
                    if n == 0 and before is not None:
                        output_graph(before, PAIRS - 1)
                    if n <= 1 and before is not None:
                        output_attended(before, HALVES[n])
                    if n >= PAIRS:
                        layer1(b, n - PAIRS)
                    if n >= 2:
                        differences(b, n - 2)
                        degrees(b, n - 2)
                    if n == 3 and before is not None:
                        output_natural(before)
                layer2_in(b, 0)

            def phase2(b, before, after):
                output_start(b, before)
                for n in range(2, PAIRS + 2):
                    if n < PAIRS:
                        layer1(b, n)
                    if n - 1 < PAIRS:
                        layer2_in(b, n - 1)
                    layer2(b, n - 2)
                    if n >= 3:
                        output_graph(b, n - 3)
                    if after is None:
                        if n == 7:
                            block_transposed(0)
                        if n == 8:
                            logits(0)
                    else:
                        if n == 7:
                            d_a.wait(pe, b, PAIRS)
                            x_transposed(after)
                        if n == 8:
                            a_f1.wait(pe, b, PAIRS)
                            values(after, 0)
                            values(after, 1)
                        if n == 9:
                            values(after, 2)
                            values(after, 3)
                            queries_keys(after, 0)

            def block_transposed(k):
                d_st.wait(pe, k, NORMED)
                if isinstance(k, int) and k == 0:
                    d_a.wait(pe, BATCHES - 1, PAIRS)
                for t in range(BT):
                    mm = nc.tensor.transpose(bank[6][:, xt(t)], z4[:, t, :], ident[:, :])
                mm.then_inc(s_zt.sem, 1)

            def logits(k):
                a_zt.wait(pe, k, 1)
                for t in range(BT):
                    mm = product(bank[6][:, t * EXPERTS:(t + 1) * EXPERTS], zT[:, xt(t)], rtT[:, :], True, True)
                mm.then_inc(s_lg.sem, 1)

            def gate_up(k, e, c):
                i = e * NC + c
                at_, n = CHUNKS[c]
                for part, o, done in ((0, bank[i % 2], s_gt), (1, bank[2 + i % 2], s_up)):
                    cols = slice(part * HID + at_, part * HID + at_ + n)
                    if part == 0 and i >= 2:
                        a_sg.wait(pe, k, i - 1)
                    if part == 1 and i >= 2:
                        d_h.wait(pe, k, i - 1)
                    z = zt[:, bass.ds(k, 1), :, :].rearrange("p o h n -> p (o h) n")
                    product3(o[0:n, :], gu_hi[:, e, cols], gu_lo[:, e, cols],
                             z[:, 0, :], z[:, 1, :]).then_inc(done.sem, 1)

            def down(k, e):
                d_h.wait(pe, k, (e + 1) * NC)
                if e >= 2:
                    d_acc.wait(pe, k, e - 1)
                for t in range(BT):
                    for c, (_, n) in enumerate(CHUNKS):
                        mm = product(bank[4 + e % 2][:, xt(t)], hT[0:n, e % 2, c, xt(t)], dn[0:n, e, c, :],
                                     c == 0, c == NC - 1)
                mm.then_inc(s_dn.sem, 1)

            def experts(k, first, after):
                a_zt.wait(pe, k, 1)
                d_zl.wait(pe, k, 1)
                if first:
                    a_f1.wait(pe, BATCHES - 1, PAIRS)
                    d_g1.wait(pe, BATCHES - 1, PAIRS)
                    d_z2.wait(pe, BATCHES - 1, PAIRS)
                for e in range(EXPERTS):
                    if first:
                        pe.wait_ge(k_gu, 2 * (e + 1))
                    for c in range(NC):
                        gate_up(k, e, c)
                        if first and (e, c) == (0, 0):
                            output_natural(BATCHES - 1)
                        if c == 0 and e >= 1:
                            if first and e == 1:
                                pe.wait_ge(w_dn, 16 * NC)
                            down(k, e - 1)
                        if (e, c) == (5, 1) and after is not None:
                            block_transposed(after)
                        if (e, c) == (6, 1) and after is not None:
                            logits(after)
                down(k, EXPERTS - 1)

            prepare_weights()
            x_transposed(0)
            pe.wait_ge(k_dve, 8)
            for c in range(4):
                values(0, c)
            queries_keys(0, 0)
            phase1(0, None)
            phase2(0, None, 1)
            phase1(1, 0)
            with pe.Fori(1, BATCHES - 1) as b:
                phase2(b, b - 1, b + 1)
                phase1(b + 1, b)
            phase2(BATCHES - 1, BATCHES - 2, None)
            output_graph(BATCHES - 1, PAIRS - 1)
            for half_ in HALVES:
                output_attended(BATCHES - 1, half_)

            experts(0, True, 1)
            with pe.Fori(1, BLOCKS - 1) as k:
                experts(k, False, k + 1)
            experts(BLOCKS - 1, False, None)

        @block.scalar
        def _(act):
            def copy(o, i, **more):
                return nc.scalar.activation(o, i, ACT.Copy, **more)

            def prepare_weights():
                act.wait_ge(k_pe, 2)
                copy(lwo[:, 0:4, :], bank[2][:, :].rearrange("p (g n) -> p g n", g=4))
                copy(lwo[:, 4:8, :], bank[3][:, :].rearrange("p (g n) -> p g n", g=4))
                act.wait_ge(k_pe, 3)
                copy(yb[:, :], bank[5][:, 0:1]).then_inc(k_act, 1)

            def x_high(b, earlier):
                s_xt.wait(act, b, 1)
                if earlier is not None:
                    s_f1.wait(act, earlier, PAIRS)
                copy(xt_hi[:, :], bank[6][:, 0:TOKENS], scale=gin[:, :]).then_inc(a_xt.sem, 1)

            def values(b, c):
                s_v.wait(act, b, c + 1)
                t, h = c // 2, c % 2
                copy(vnat[:, t, h * 512:(h + 1) * 512], bank[c % 2][:, :]).then_inc(a_v.sem, 1)

            def queries_keys(b, n):
                s_qk.wait(act, b, n + 1)
                copy(qT[:, n % 2, :], bank[0][:, 0:TOKENS])
                for a in range(2):
                    rows = slice(a * DHEAD, (a + 1) * DHEAD)
                    done = copy(kT[rows, n % 2, a, :], bank[0][rows, TOKENS:], scale=SCALE)
                done.then_inc(a_qk.sem, 1)

            def exps(b, n, t):
                d_max.wait(act, b, 2 * n + 1 + t)
                s, width = n % 3, (t + 1) * P
                e = eb if t else ea
                for a in range(2):
                    i = 2 * t + a
                    done = nc.scalar.activation(e[:, s, a, :], bank[1 + t][:, a * width:(a + 1) * width], ACT.Exp,
                                                bias=nmax[:, s, i:i + 1], accum_out=ssum[:, s, i:i + 1])
                done.then_inc(a_exp.sem, 1)

            def graph(b, n):
                s_t.wait(act, b, n + 1)
                copy(gt0[:, n, :, :], bank[3][:, :].rearrange("p (a i) -> p a i", a=2))
                copy(gt1[:, n, :, :], bank[4][:, 0:2 * P].rearrange("p (a i) -> p a i", a=2)).then_inc(a_gt.sem, 1)

            def differences(b, n):
                s_d.wait(act, b, n + 1)
                copy(dT[:, n, :], bank[5][:, 0:TOKENS]).then_inc(a_d.sem, 1)

            def gelu1(b, n):
                s_f1.wait(act, b, n + 1)
                nc.scalar.activation(f1T[:, n % 4, :], bank[n % 2][:, 0:TOKENS], ACT.Gelu,
                                     bias=gb[:, 0:1]).then_inc(a_f1.sem, 1)

            def gelu2(b, n):
                d_z2.wait(act, b, n + 1)
                nc.scalar.activation(f2T[:, n % 2, :], z2[:, n % 2, :], ACT.Gelu,
                                     bias=gb[:, 1:2]).then_inc(a_f2.sem, 1)

            def phase1(b):
                for n in range(PAIRS + 2):
                    if n >= 2:
                        graph(b, n - 2)
                    if n + 1 < PAIRS:
                        queries_keys(b, n + 1)
                    if n < PAIRS:
                        exps(b, n, 0)
                        exps(b, n, 1)
                    if n >= PAIRS:
                        gelu1(b, n - PAIRS)
                    if n >= 2:
                        differences(b, n - 2)

            def phase2(b, after):
                for n in range(2, PAIRS + 2):
                    if n < PAIRS:
                        gelu1(b, n)
                    if n == 8 and after is not None:
                        x_high(after, b)
                    gelu2(b, n - 2)
                    if after is not None and n == 9:
                        for c in range(4):
                            values(after, c)
                        queries_keys(after, 0)
                    if after is None and n == 7:
                        block_transposed(0)

            def block_transposed(k):
                s_zt.wait(act, k, 1)
                copy(zT[:, :], bank[6][:, :], scale=normw[:, :]).then_inc(a_zt.sem, 1)

            def shares(k):
                d_st.wait(act, k, GAP)
                nc.scalar.activation(th[:, :], gap[:, :], ACT.Tanh, scale=0.5).then_inc(a_th.sem, 1)

            def experts(k, after):
                for i in range(EXPERTS * NC):
                    n = CHUNKS[i % NC][1]
                    s_gt.wait(act, k, i + 1)
                    if i >= 2:
                        d_h.wait(act, k, i - 1)
                    nc.scalar.activation(sg[0:n, i % 2, :], bank[i % 2][0:n, :], ACT.Silu).then_inc(a_sg.sem, 1)
                    if after is not None and i == 5 * NC + 2:
                        block_transposed(after)
                    if after is not None and i == 7 * NC:
                        shares(after)

            act.wait_ge(w_small, SMALL_ALL)
            act.wait_ge(k_pool, 2)
            prepare_weights()
            x_high(0, None)
            for c in range(4):
                values(0, c)
            queries_keys(0, 0)
            phase1(0)
            with act.Fori(0, BATCHES - 2) as b:
                phase2(b, b + 1)
                phase1(b + 1)
            phase2(BATCHES - 2, BATCHES - 1)
            phase1(BATCHES - 1)
            phase2(BATCHES - 1, None)

            shares(0)
            with act.Fori(0, BLOCKS - 1) as k:
                experts(k, k + 1)
            experts(BLOCKS - 1, None)

        @block.vector
        def _(dve):
            V = nc.vector

            def prepare_weights():
                dve.wait_ge(k_pool, 3)
                V.tensor_copy(ident_bf[:, :], ident[:, :])
                for a in range(2):
                    V.tensor_copy(mask[:, a, :], maskf[:, :])
                dve.wait_ge(w_small, SMALL_ALL)
                V.tensor_tensor(gwi[:, :], gw[:, 0, :], ident[:, :], ALU.add).then_inc(k_dve, 1)
                dve.wait_ge(w_w, 5 * 16)
                V.tensor_copy(v_hi[:, :], raw[:, 2, :])
                for n in range(2):
                    V.tensor_copy(w_hi[:, n, :], raw[:, n, :])
                V.tensor_scalar(w_hi[:, 2, :], raw[:, 2, :], -1.0, None, ALU.mult).then_inc(k_dve, 1)
                dve.wait_ge(k_dve, 2)
                V.tensor_tensor(v_lo[:, :], raw[:, 2, :], v_hi[:, :].bitcast(f32), ALU.subtract)
                for n in range(2):
                    V.tensor_tensor(w_lo[:, n, :], raw[:, n, :], w_hi[:, n, :].bitcast(f32), ALU.subtract)
                V.scalar_tensor_tensor(w_lo[:, 2, :], raw[:, 2, :], -1.0, w_hi[:, 2, :].bitcast(f32),
                                       ALU.mult, ALU.subtract).then_inc(k_dve, 1)
                dve.wait_ge(k_pe, 1)
                for h in range(2):
                    V.tensor_copy(mv_hi[:, h * 512:(h + 1) * 512], bank[h][:, :]).then_inc(k_dve, 1)
                dve.wait_ge(k_dve, 5)
                for h in range(2):
                    cols = slice(h * 512, (h + 1) * 512)
                    V.tensor_tensor(mv_lo[:, cols], bank[h][:, :], mv_hi[:, cols].bitcast(f32),
                                    ALU.subtract)
                dve.wait_ge(k_pe, 3)
                V.tensor_copy(cy_hi[:, :], bank[4][:, 0:P]).then_inc(k_dve, 1)
                dve.wait_ge(k_dve, 6)
                V.tensor_tensor(cy_lo[:, :], bank[4][:, 0:P], cy_hi[:, :].bitcast(f32),
                                ALU.subtract).then_inc(k_dve, 1)
                dve.wait_ge(k_act, 1)
                dve.wait_ge(k_dve, 7)
                V.tensor_scalar(alph[:, :], alph[:, :], -0.5, 2.0, ALU.max, ALU.min).then_inc(k_dve, 1)

            def wait_ahead(signal, turn, k):
                signal.wait(dve, turn, k)
                V.memset(hold[:, :], 0.0)

            def stats(b, src, step):
                for t in range(TILES):
                    done = V.bn_stats(stat[:, t, :], src(t))
                done.then_inc(d_ln.sem, 1)

            def aggregate(b, step):
                wait_ahead(d_ln, b, step)
                for t in range(TILES):
                    done = V.bn_aggr(mv_[:, t, :], stat[:, t, :])
                done.then_inc(d_ln.sem, 1)
                d_ln.wait(dve, b, step + 1)
                V.tensor_scalar(ve[:, :], mv_[:, :, 1], EPS_LN, None, ALU.add).then_inc(d_ln.sem, 1)

            def normalise(b, step, power, o, src):
                p_ln.wait(dve, b, power)
                for t in range(TILES):
                    done = V.tensor_scalar(o[:, t, :], src(t), mv_[:, t, 0:1], rstd[:, t:t + 1],
                                           ALU.subtract, ALU.mult)
                done.then_inc(d_ln.sem, 1)

            def x_tile(b):
                return lambda t: x_all[:, bass.ds(b * TILES + t, 1), :].rearrange("p o d -> p (o d)")

            def norm_step(b, i):
                if i == 0:
                    stats(b, x_tile(b), 0)
                if i == 1:
                    aggregate(b, 1)
                if i == 2:
                    normalise(b, 3, 1, xh, x_tile(b))
                if i == 3:
                    wait_ahead(d_ln, b, 4)
                    stats(b, lambda t: xh[:, t, :], 4)
                if i == 4:
                    aggregate(b, 5)
                if i == 5:
                    normalise(b, 7, 2, xn, lambda t: xh[:, t, :])

            def x_low(b):
                a_xt.wait(dve, b, 1)
                V.scalar_tensor_tensor(xt_lo[:, :], bank[6][:, 0:TOKENS], gin[:, :],
                                       xt_hi[:, :].bitcast(f32), ALU.mult, ALU.subtract).then_inc(d_xt.sem, 1)

            def maxima(b, n):
                for t in range(2):
                    s_s.wait(dve, b, 2 * n + 1 + t)
                    width = (t + 1) * P
                    V.tensor_reduce(nmax[:, n % 3, 2 * t:2 * t + 2],
                                    bank[1 + t][:, 0:2 * width].rearrange("p (a j) -> p a j", a=2), X, ALU.max,
                                    negate=True).then_inc(d_max.sem, 1)

            def adjacency(b, n):
                s = n % 3
                a_exp.wait(dve, b, 2 * n + 2)
                V.reciprocal(rs[:, s, :], ssum[:, s, :])
                for a in range(2):
                    V.scalar_tensor_tensor(ea[:, s, a, :], ident[:, :], ssum[:, s, a:a + 1], ea[:, s, a, :],
                                           ALU.mult, ALU.max, accum_out=den[:, s, a:a + 1])
                for a in range(2):
                    done = V.scalar_tensor_tensor(eb[:, s, a, :], idw[:, :], ssum[:, s, 2 + a:3 + a],
                                                  eb[:, s, a, :], ALU.mult, ALU.max,
                                                  accum_out=den[:, s, 2 + a:3 + a])
                done.then_inc(d_e.sem, 1)
                d_e.wait(dve, b, n + 1)
                V.reciprocal(wgt[:, s, :], den[:, s, :]).then_inc(d_w.sem, 1)

            def attended(b, n):
                s_deg.wait(dve, b, n + 1)
                a_d.wait(dve, b, n + 1)
                V.tensor_tensor(aT[:, n, :], bank[6][:, 0:TOKENS], dT[:, n, :], ALU.mult).then_inc(d_a.sem, 1)

            def output_bias(b):
                s_y.wait(dve, b, 1)
                V.tensor_scalar(yT[:, :], bank[7][:, 0:TOKENS], yb[:, :], None, ALU.add).then_inc(d_yT.sem, 1)

            def output_kept(b):
                s_yn.wait(dve, b, 1)
                V.tensor_copy(y_all[:, tokens(b), :],
                              bank[7][:, 0:TOKENS].rearrange("p (t d) -> p t d", t=TILES)).then_inc(d_y.sem, 1)

            def phase1(b, before):
                for n in range(PAIRS + 2):
                    if 0 <= n - 1 < PAIRS:
                        adjacency(b, n - 1)
                    if n < PAIRS:
                        maxima(b, n)
                    if n >= 3:
                        attended(b, n - 3)
                    if n == 2 and before is not None:
                        output_bias(before)
                    if n == 4 and before is not None:
                        output_kept(before)
                attended(b, PAIRS - 1)

            def layer2_in(b, n):
                s_g1.wait(dve, b, n + 1)
                V.tensor_copy(g1[:, n % 2, :, :],
                              bank[2 + n % 2][:, 0:TOKENS].rearrange("p (t d) -> p t d", t=TILES)).then_inc(d_g1.sem, 1)

            def layer2_out(b, n):
                s_h2.wait(dve, b, n + 1)
                V.tensor_tensor(z2[:, n % 2, :], bank[4 + n % 2][:, 0:TOKENS], f1T[:, n % 4, :],
                                ALU.add).then_inc(d_z2.sem, 1)

            def phase2(b, after):
                layer2_in(b, 0)
                for n in range(2, PAIRS + 2):
                    if n - 1 < PAIRS:
                        layer2_in(b, n - 1)
                    if n == 8 and after is not None:
                        x_low(after)
                    layer2_out(b, n - 2)
                    if after is not None:
                        norm_step(after, n - 2)
                    else:
                        split_gate_up(n - 2)
                        for step in range(2 * n - 4, min(2 * n - 2, 12)):
                            norm_tokens(0, step)

            def split_gate_up(e):
                dve.wait_ge(w_gu[e % 2], 16 * (e // 2 + 1))
                V.tensor_copy(gu_hi[:, e, :], raw_gu[:, e % 2, :]).then_inc(k_gu, 1)
                dve.wait_ge(k_gu, 2 * e + 1)
                V.tensor_tensor(gu_lo[:, e, :], raw_gu[:, e % 2, :], gu_hi[:, e, :].bitcast(f32),
                                ALU.subtract).then_inc(k_gu, 1)

            class Steps:

                def __init__(self, k, n):
                    self.k, self.n = k, n

                def done(self, ins):
                    self.n += 1
                    ins.then_inc(d_st.sem, 1)

                def ready(self):
                    d_st.wait(dve, self.k, self.n)

                def ready_ahead(self):
                    wait_ahead(d_st, self.k, self.n)

            def norm_tokens(k, step):
                now = bass.ds(k * BT, BT)
                x1 = x_all[:, now, :]

                def tile(whole, t):
                    return whole[:, bass.ds(k * BT + t, 1), :].rearrange("p o d -> p (o d)")

                def moments(src, s):
                    if s.n:
                        s.ready_ahead()
                    for t in range(BT):
                        last = V.bn_stats(st4[:, t, :], tile(src, t))
                    s.done(last)

                def variances(s):
                    s.ready_ahead()
                    for t in range(BT):
                        last = V.bn_aggr(mv4[:, t, :], st4[:, t, :])
                    s.done(last)
                    s.ready()
                    s.done(V.tensor_scalar(ve4[:, :], mv4[:, :, 1], EPS_LN, None, ALU.add))

                def normalised(src, s, power):
                    p_st.wait(dve, k, power)
                    for t in range(BT):
                        last = V.tensor_scalar(t4[:, t, :], tile(src, t), mv4[:, t, 0:1], rs4[:, t:t + 1],
                                               ALU.subtract, ALU.mult)
                    s.done(last)

                if step == 0:
                    moments(y_all, Steps(k, 0))
                elif step == 1:
                    variances(Steps(k, 1))
                elif step == 2:
                    normalised(y_all, Steps(k, 3), 1)
                elif step == 3:
                    s = Steps(k, 4)
                    s.ready()
                    s.done(V.tensor_tensor(t4[:, :, :], t4[:, :, :],
                                           gout[:, :].unsqueeze(1).to_broadcast([P, BT, DIM]), ALU.mult))
                elif step == 4:
                    s = Steps(k, 5)
                    s.ready()
                    s.done(V.tensor_tensor(x1, x1, t4[:, :, :], ALU.add))
                elif step == 5:
                    moments(x_all, Steps(k, 6))
                elif step == 6:
                    variances(Steps(k, 7))
                elif step == 7:
                    normalised(x_all, Steps(k, 9), 2)
                elif step == 8:
                    s = Steps(k, 10)
                    s.ready()
                    s.done(V.tensor_tensor(x1, x1, t4[:, :, :], ALU.add))
                elif step == 9:
                    s = Steps(k, 11)
                    for t in range(BT):
                        last = V.scalar_tensor_tensor(sq4[:, t, :], t4[:, t, :], 1.0, t4[:, t, :], ALU.mult,
                                                      ALU.mult, accum_out=ss4[:, t:t + 1])
                    s.done(last)
                elif step == 10:
                    s = Steps(k, 12)
                    s.ready()
                    s.done(V.tensor_scalar(ve4[:, :], ss4[:, :], 1.0 / DIM, EPS_RMS, ALU.mult, ALU.add))
                elif step == 11:
                    p_st.wait(dve, k, 3)
                    s = Steps(k, 13)
                    for t in range(BT):
                        last = V.tensor_scalar(z4[:, t, :], t4[:, t, :], rs4[:, t:t + 1], None, ALU.mult)
                    s.done(last)
                    assert s.n == NORMED

            def z_split(k):
                s = Steps(k, NORMED)
                a_zt.wait(dve, k, 1)
                s.ready()
                z = zt[:, bass.ds(k, 1), :, :].rearrange("p o h n -> p (o h) n")
                s.done(V.tensor_copy(z[:, 0, :], zT[:, :]))
                s.ready()
                V.tensor_tensor(z[:, 1, :], zT[:, :], z[:, 0, :].bitcast(f32), ALU.subtract).then_inc(d_zl.sem, 1)
                assert s.n == SPLIT

            def best_two(k):
                s = Steps(k, SPLIT)
                s_lg.wait(dve, k, 1)
                s.done(V.tensor_copy(lg[:, :, :], bank[6][:, 0:BT * EXPERTS].rearrange("p (t e) -> p t e", t=BT)))
                s.ready_ahead()
                for t in range(BT):
                    last = V.max(top[:, t, :], lg[:, t, :])
                s.done(last)
                s.ready()
                s.done(V.tensor_tensor(gap[:, :], top[:, :, 0], top[:, :, 1], ALU.subtract))
                for t in range(BT):
                    last = V.max_index(topi[:, t, :], top[:, t, :], lg[:, t, :])
                s.done(last)
                s.ready()
                s.done(V.tensor_copy(topf[:, :, :], topi[:, :, 0:2]))
                s.ready()
                for r in range(2):
                    last = V.tensor_tensor(eq[:, r, :, :], iot[:, :].unsqueeze(1).to_broadcast([P, BT, EXPERTS]),
                                           topf[:, :, r:r + 1].to_broadcast([P, BT, EXPERTS]), ALU.is_equal)
                s.done(last)
                assert s.n == CHOSEN

            def shares(k):
                s = Steps(k, CHOSEN)
                a_th.wait(dve, k, 1)
                V.tensor_scalar(wt2[:, 0, :], th[:, :], 1.0, 0.5, ALU.add, ALU.mult)
                s.done(V.tensor_scalar(wt2[:, 1, :], th[:, :], -0.5, 0.5, ALU.mult, ALU.add))
                s.ready()
                s.done(V.tensor_scalar(wt2[:, :, :], wt2[:, :, :], alph[:, :], None, ALU.mult))
                s.ready()
                for r in range(2):
                    last = V.tensor_tensor(eq[:, r, :, :], eq[:, r, :, :],
                                           wt2[:, r, :].unsqueeze(2).to_broadcast([P, BT, EXPERTS]), ALU.mult)
                s.done(last)
                s.ready()
                V.tensor_tensor(comb[:, bass.ds(k, 1), :, :].rearrange("p o t e -> p (o t) e"), eq[:, 0, :, :],
                                eq[:, 1, :, :], ALU.add).then_inc(d_comb.sem, 1)
                assert s.n == d_st.per == ROUTED

            def hidden(k, i):
                e, c = i // NC, i % NC
                n = CHUNKS[c][1]
                a_sg.wait(dve, k, i + 1)
                s_up.wait(dve, k, i + 1)
                if c == 0 and e >= 2:
                    s_dn.wait(dve, k, e - 1)
                V.tensor_tensor(hT[0:n, e % 2, c, :], bank[2 + i % 2][0:n, :], sg[0:n, i % 2, :],
                                ALU.mult).then_inc(d_h.sem, 1)

            def add_expert(k, slot, e):
                s_dn.wait(dve, k, e + 1)
                if e > 0:
                    d_acc.wait(dve, k, e)
                for t in range(BT):
                    into = acc[:, slot, t, :]
                    w = comb[:, bass.ds(k, 1), t, e:e + 1].rearrange("p o e -> p (o e)")
                    src = x_all[:, bass.ds(k * BT + t, 1), :].rearrange("p o d -> p (o d)") if e == 0 else into
                    last = V.scalar_tensor_tensor(into, bank[4 + e % 2][:, xt(t)], w, src, ALU.mult, ALU.add)
                last.then_inc(d_acc.sem, 1)

            def experts(k, slot, after, turn=None):
                d_comb.wait(dve, k, 1)
                if turn is not None:
                    o_out[slot].wait(dve, turn, 0)
                for e in range(EXPERTS):
                    for c in range(NC):
                        i = e * NC + c
                        hidden(k, i)
                        if c == 1 and e > 0:
                            add_expert(k, slot, e - 1)
                        if isinstance(k, int) and k == 0 and i == 0:
                            output_kept(BATCHES - 1)
                        if after is not None:
                            if 1 <= i <= 12:
                                norm_tokens(after, i - 1)
                            if i == 18:
                                z_split(after)
                            if i == 20:
                                best_two(after)
                            if i == 23:
                                shares(after)
                add_expert(k, slot, EXPERTS - 1)

            dve.wait_ge(w_x0, 16)
            for i in range(6):
                norm_step(0, i)
            prepare_weights()
            x_low(0)
            phase1(0, None)
            dve.wait_ge(w_x, 16)
            with dve.Fori(0, BATCHES - 2) as b:
                phase2(b, b + 1)
                phase1(b + 1, b)
            phase2(BATCHES - 2, BATCHES - 1)
            phase1(BATCHES - 1, BATCHES - 2)
            phase2(BATCHES - 1, None)
            z_split(0)
            best_two(0)
            output_bias(BATCHES - 1)
            shares(0)
            experts(0, 0, 1)
            experts(1, 1, 2)
            with dve.Fori(1, BLOCKS // 2 - 1) as i:
                experts(i * 2, 0, i * 2 + 1, turn=i)
                experts(i * 2 + 1, 1, i * 2 + 2, turn=i)
            experts(BLOCKS - 2, 0, BLOCKS - 1, turn=BLOCKS // 2 - 1)
            experts(BLOCKS - 1, 1, None, turn=BLOCKS // 2 - 1)


def kernel(**inputs):
    import numpy as np
    import concourse.bacc as bacc
    from concourse.bass_utils import run_bass_kernel_spmd

    a = {n[3:]: np.asarray(v) for n, v in inputs.items()}
    given = dict(
        x=a["attn_x"].reshape(ALL, DIM), wq=a["attn_Wq"], wk=a["attn_Wk"], wv=a["attn_Wv"],
        wvT=a["attn_Wv"].T, gnn_w=a["attn_gnn_w"], gnn_b=a["attn_gnn_b"], lin_wT=a["attn_lin_w"].T,
        lin_b=a["attn_lin_b"].reshape(DHEAD, 1), wo=a["attn_Wo"], gamma_in=a["attn_gamma_in"].reshape(DIM, 1),
        gamma_out=a["attn_gamma_out"].reshape(1, DIM), norm_w=a["ffn_norm_weight"].reshape(DIM, 1),
        routerT=a["ffn_router_weight"].T, guT=a["ffn_gate_up_weight"].transpose(0, 2, 1),
        downT=a["ffn_down_weight"].transpose(0, 2, 1), alpha=a["ffn_residual_alpha"].reshape(1, 1))
    given = {n: np.ascontiguousarray(v) for n, v in given.items()}
    nc = bacc.Bacc("TRN2", target_bir_lowering=False, num_devices=1)
    args = {n: nc.dram_tensor(f"in_{n}", v.shape, f32, kind="ExternalInput").ap() for n, v in given.items()}
    out = nc.dram_tensor("out", (ALL, DIM), f32, kind="ExternalOutput").ap()
    build_program(nc, out=out, **args)
    r = run_bass_kernel_spmd(nc, [{f"in_{n}": v for n, v in given.items()}], core_ids=[0])
    return r.results[0]["out"].reshape(BATCHES, TOKENS, DIM)
```

```python
from contextlib import ExitStack

import concourse.bass as bass
from concourse import mybir

P = 128
BATCHES, TOKENS, DIM = 16, 256, 128
HEADS, DHEAD = 16, 64
PAIRS = HEADS // 2
TILES = TOKENS // P
HD = HEADS * DHEAD
ALL = BATCHES * TOKENS
EXPERTS, HID = 8, 352
SORTED = BATCHES - 2
KEPT = BATCHES - SORTED
BT = KEPT * TILES
BLOCK = BT * P
CHOICES = 2
SIDE = TILES * CHOICES
ROOM = SORTED * TILES
STEPS = SORTED * SIDE + EXPERTS
UNROLL = 4
GROUPS = STEPS // UNROLL
SLOT_ROWS = (EXPERTS * ROOM + EXPERTS) * P
CLEAR = 8
CHUNKS = [(c, min(P, HID - c)) for c in range(0, HID, P)]
NC = len(CHUNKS)
EPS_LN, EPS_RMS = 1e-5, 1e-6
MASKED = -3.0e38
SCALE = DHEAD ** -0.5

f32, f32r, bf16, u32 = mybir.dt.float32, mybir.dt.float32r, mybir.dt.bfloat16, mybir.dt.uint32
ALU = mybir.AluOpType
ACT = mybir.ActivationFunctionType
X = mybir.AxisListType.X


assert STEPS % UNROLL == 0 and SLOT_ROWS % (CLEAR * P) == 0


class Signal:

    def __init__(self, sem, per):
        self.sem, self.per = sem, per

    def wait(self, engine, turn, k):
        engine.wait_ge(self.sem, turn * self.per + k)


def build_program(nc, x, wq, wk, wv, wvT, gnn_w, gnn_b, lin_wT, lin_b, wo, gamma_in, gamma_out,
                  norm_w, routerT, guT, downT, alpha, slots, out):
    ctx = ExitStack()
    attn = ExitStack()

    def sb(name, shape, dt=f32, where=ctx):
        return where.enter_context(nc.sbuf_tensor(name, shape, dt))

    def sem(name):
        return ctx.enter_context(nc.semaphore(name))

    with ctx:
        bank = [ctx.enter_context(nc.psum_tensor(f"bank{i}", [P, 512], f32)) for i in range(8)]

        x_all = sb("x_all", [P, BATCHES * TILES, DIM])
        y_all = sb("y_all", [P, BATCHES * TILES, DIM])
        ident = sb("ident", [P, P])
        half = sb("half", [P, TILES])
        gout = sb("gout", [P, DIM])
        normw = sb("normw", [P, 1])
        hold = sb("hold", [P, 1])
        rtT = sb("rtT", [P, EXPERTS])
        alph = sb("alph", [P, 1])

        lb = sb("lb", [P, 1])
        gin = sb("gin", [P, 1])
        yb = sb("yb", [P, 1])
        yT = sb("yT", [P, TOKENS])
        zT = sb("zT", [P, TOKENS])
        st4 = sb("st4", [P, TILES, 6])
        mv4 = sb("mv4", [P, TILES, 2])
        ve4 = sb("ve4", [P, TILES])
        rs4 = sb("rs4", [P, TILES])
        t4 = sb("t4", [P, TILES, DIM])
        z4 = sb("z4", [P, TILES, DIM])
        sq4 = sb("sq4", [P, TILES, DIM])
        ss4 = sb("ss4", [P, TILES])
        lg = sb("lg", [P, TILES, EXPERTS])
        top = sb("top", [P, TILES, 8])
        topi = sb("topi", [P, TILES, 8], u32)
        topf = sb("topf", [P, TILES, CHOICES])
        iot = sb("iot", [P, EXPERTS])
        gap = sb("gap", [P, TILES])
        ratio = sb("ratio", [P, TILES])
        ratio1 = sb("ratio1", [P, TILES])
        share = sb("share", [P, BATCHES, CHOICES, TILES])
        eq = sb("eq", [P, CHOICES, TILES, EXPERTS])
        eq_bf = sb("eq_bf", [P, SIDE + 1, EXPERTS], bf16)
        zero = sb("zero", [P, CLEAR * DIM])
        comb = sb("comb", [P, BT, EXPERTS])
        before_bf = sb("before_bf", [P, P], bf16)
        ones_bf = sb("ones_bf", [P, P], bf16)
        first_row = sb("first_row", [P, EXPERTS])
        next_row = sb("next_row", [P, EXPERTS])
        place = sb("place", [P, SIDE, EXPERTS])
        row_f = sb("row_f", [P, SIDE])
        row_now = sb("row_now", [P, SIDE], u32)
        row_all = sb("row_all", [P, SORTED, SIDE], u32)
        tile_from = sb("tile_from", [P, ROOM])
        step_no = sb("step_no", [P, STEPS])
        upto = sb("upto", [P, EXPERTS, EXPERTS])
        used = sb("used", [P, EXPERTS])
        tiles_used = sb("tiles_used", [P, EXPERTS])
        last_step = sb("last_step", [P, EXPERTS])
        unused = sb("unused", [P, EXPERTS])
        passed_by = sb("passed_by", [P, EXPERTS, EXPERTS])
        taken = sb("taken", [P, EXPERTS, ROOM])
        passed = sb("passed", [P, STEPS, EXPERTS])
        step_f = sb("step_f", [P, 2, STEPS])
        step_expert = sb("step_expert", [P, STEPS], u32)
        step_row = sb("step_row", [P, STEPS], u32)

        zin = sb("zin", [P, UNROLL, DIM])
        sz_hi = sb("sz_hi", [P, 2, P], f32r)
        sz_lo = sb("sz_lo", [P, 2, P], f32r)
        shid = sb("shid", [P, 2, NC * P])

        def at(name, shape, dt=f32):
            return sb(name, shape, dt, attn)

        raw = at("raw", [P, 3, HD])
        wvt = at("wvt", [P, PAIRS, P])
        linT = at("linT", [P, P])
        maskf = at("maskf", [P, P])
        before_f = at("before_f", [P, P])
        w_hi = at("w_hi", [P, 2, HD], f32r)
        w_lo = at("w_lo", [P, 2, HD], f32r)
        v_hi = at("v_hi", [P, HD], f32r)
        v_lo = at("v_lo", [P, HD], f32r)
        vnat = at("vnat", [P, TILES, HD])
        ea = at("ea", [P, 3, 2, P])
        eb = at("eb", [P, 3, 2, 2 * P])
        deg = at("deg", [P, 3, 4, DHEAD])
        qT = at("qT", [P, 2, TOKENS])
        kT = at("kT", [P, 2, 2, TOKENS])
        gt0 = at("gt0", [P, PAIRS, 2, TOKENS])
        gt1 = at("gt1", [P, PAIRS, 2, P])
        gvT = at("gvT", [P, PAIRS, TOKENS])
        vT = at("vT", [P, PAIRS, TOKENS])
        aT = at("aT", [P, PAIRS, TOKENS])
        f1T = at("f1T", [P, 4, TOKENS])
        g1 = at("g1", [P, 2, TILES, P])
        dT = at("dT", [P, TOKENS])
        z1 = at("z1", [P, 2, TOKENS])
        z2 = at("z2", [P, 2, TOKENS])
        f2T = at("f2T", [P, 2, TOKENS])
        wo_sb = at("wo_sb", [P, PAIRS, P])
        gw = at("gw", [P, 2, P])
        gb = at("gb", [P, 2])
        cy_hi = at("cy_hi", [P, P], f32r)
        cy_lo = at("cy_lo", [P, P], f32r)
        lwo = at("lwo", [P, PAIRS, P])
        ident_bf = at("ident_bf", [P, P], bf16)
        mask = at("mask", [P, 2, P], bf16)
        idw = at("idw", [P, 2 * P])
        stat = at("stat", [P, TILES, 6])
        mv_ = at("mv_", [P, TILES, 2])
        ve = at("ve", [P, TILES])
        rstd = at("rstd", [P, TILES])
        xh = at("xh", [P, TILES, DIM])
        xn = at("xn", [P, TILES, DIM])
        xt_hi = at("xt_hi", [P, TOKENS], f32r)
        xt_lo = at("xt_lo", [P, TOKENS], f32r)
        nmax = at("nmax", [P, 3, 4])
        ssum = at("ssum", [P, 3, 4])
        den = at("den", [P, 3, 4])
        rs = at("rs", [P, 3, 4])
        wgt = at("wgt", [P, 3, 4])
        attn.close()

        raw_gu = sb("raw_gu", [P, 2, 2 * HID])
        dn = sb("dn", [P, EXPERTS, NC, DIM])
        gu_hi = sb("gu_hi", [P, EXPERTS, 2 * HID], f32r)
        gu_lo = sb("gu_lo", [P, EXPERTS, 2 * HID], f32r)
        ssg = sb("ssg", [P, 2, HID])
        shT = sb("shT", [P, 2, NC, P])
        zt = sb("zt", [P, 2, BLOCK], f32r)
        zout = sb("zout", [P, UNROLL, DIM])
        got = sb("got", [P, UNROLL, CHOICES, DIM])
        hT = sb("hT", [P, 2, NC, BLOCK])
        sg = sb("sg", [P, 2, BLOCK])
        acc = sb("acc", [P, BT, DIM])

        w_x0, w_x, w_w, w_small = sem("w_x0"), sem("w_x"), sem("w_w"), sem("w_small")
        w_gu = [sem(f"w_gu{i}") for i in range(2)]
        w_dn = sem("w_dn")
        k_pool, k_dve, k_pe, k_act = sem("k_pool"), sem("k_dve"), sem("k_pe"), sem("k_act")
        d_ln = Signal(sem("d_ln"), 8)
        p_ln = Signal(sem("p_ln"), 2)
        s_xt = Signal(sem("s_xt"), 1)
        a_xt = Signal(sem("a_xt"), 1)
        d_xt = Signal(sem("d_xt"), 1)
        s_v = Signal(sem("s_v"), 4)
        a_v = Signal(sem("a_v"), 4)
        s_qk, a_qk = Signal(sem("s_qk"), PAIRS), Signal(sem("a_qk"), PAIRS)
        s_s = Signal(sem("s_s"), 2 * PAIRS)
        d_max = Signal(sem("d_max"), 2 * PAIRS)
        a_exp = Signal(sem("a_exp"), 2 * PAIRS)
        d_e = Signal(sem("d_e"), PAIRS)
        d_w = Signal(sem("d_w"), PAIRS)
        p_deg = Signal(sem("p_deg"), PAIRS)
        p_g = Signal(sem("p_g"), PAIRS)
        s_t, a_gt = Signal(sem("s_t"), PAIRS), Signal(sem("a_gt"), PAIRS)
        s_d, a_d = Signal(sem("s_d"), PAIRS), Signal(sem("a_d"), PAIRS)
        d_d = Signal(sem("d_d"), PAIRS)
        s_deg = Signal(sem("s_deg"), PAIRS)
        d_a = Signal(sem("d_a"), PAIRS)
        s_f1, d_z1 = Signal(sem("s_f1"), PAIRS), Signal(sem("d_z1"), PAIRS)
        a_f1 = Signal(sem("a_f1"), PAIRS)
        s_g1, a_g1 = Signal(sem("s_g1"), PAIRS), Signal(sem("a_g1"), PAIRS)
        s_h2, d_z2 = Signal(sem("s_h2"), PAIRS), Signal(sem("d_z2"), PAIRS)
        a_f2 = Signal(sem("a_f2"), PAIRS)
        s_y, d_yT = Signal(sem("s_y"), 1), Signal(sem("d_yT"), 1)
        s_yn, d_y = Signal(sem("s_yn"), 1), Signal(sem("d_y"), 1)
        d_st = Signal(sem("d_st"), 14)
        p_st = Signal(sem("p_st"), 3)
        s_zt, a_zt = Signal(sem("s_zt"), 1), Signal(sem("a_zt"), 1)
        s_lg, a_ratio = Signal(sem("s_lg"), 1), Signal(sem("a_ratio"), 1)
        d_ch = Signal(sem("d_ch"), 11)
        s_pre = Signal(sem("s_pre"), 1)
        d_pl = Signal(sem("d_pl"), 6)
        z_free = Signal(sem("z_free"), 16 * SIDE)
        w_clear, d_tab, k_row, k_eq = sem("w_clear"), sem("d_tab"), sem("k_row"), sem("k_eq")
        w_zin = [Signal(sem(f"w_zin{i}"), 16) for i in range(UNROLL)]
        w_zout = [Signal(sem(f"w_zout{i}"), 16) for i in range(UNROLL)]
        s_tz, a_zh, d_zlo = Signal(sem("s_tz"), 1), Signal(sem("a_zh"), 1), Signal(sem("d_zlo"), 1)
        s_gu, a_silu, d_hid = Signal(sem("s_gu"), 1), Signal(sem("a_silu"), 1), Signal(sem("d_hid"), 1)
        s_ht, a_ht = Signal(sem("s_ht"), 1), Signal(sem("a_ht"), 1)
        s_down, d_zout = Signal(sem("s_down"), 1), Signal(sem("d_zout"), 1)
        d_zt, d_comb = sem("d_zt"), sem("d_comb")
        k_gu = sem("k_gu")
        s_gt, s_up, a_sg, d_h = sem("s_gt"), sem("s_up"), sem("a_sg"), sem("d_h")
        s_dn, d_acc = sem("s_dn"), sem("d_acc")
        w_got = [sem(f"w_got{i}") for i in range(UNROLL)]
        d_fin, w_out = sem("d_fin"), sem("w_out")

        def xt(t):
            return slice(t * P, (t + 1) * P)

        def tokens(b):
            return bass.ds(b * TILES, TILES)

        SMALL_ALL = 17 * 16
        POWERS = (3, 9, 13)
        NORMED = 14
        GAP, ONE_HOT = 3, 7
        TABLES = 11
        LOGITS, PLACES = slice(0, TILES * EXPERTS), slice(0, (SIDE + 1) * EXPERTS)
        KEPT_Z = STEPS - 4
        LATE = 2

        def step(g, i):
            return g * UNROLL + i

        def live(g, i):
            return not isinstance(g, int) or 0 <= step(g, i) < STEPS

        def turn(g, i):
            return g + i // UNROLL, i % UNROLL

        def at_step(g, i):
            return bass.ds(step(g, i), 1)

        block = ctx.enter_context(nc.Block())

        @block.sync
        def _(sp):
            xv = x.rearrange("(t p) d -> p t d", p=P)
            sp.dma_start(x_all[:, 0:TILES, :], xv[:, 0:TILES, :]).then_inc(w_x0, 16)
            for dst, src in ((gin[:, :], gamma_in), (normw[:, :], norm_w), (rtT[:, :], routerT),
                             (gout[:, :], gamma_out.to_broadcast([P, DIM])),
                             (alph[:, :], alpha.to_broadcast([P, 1]))):
                sp.dma_start(dst, src).then_inc(w_small, 16)
            for n, w in enumerate((wq, wk, wv)):
                sp.dma_start(raw[:, n, :], w).then_inc(w_w, 16)
            sp.dma_start(wvt[:, :, :], wvT.rearrange("(g p) d -> p g d", p=P)).then_inc(w_w, 16)
            sp.dma_start(wo_sb[:, :, :], wo.rearrange("(g p) d -> p g d", p=P)).then_inc(w_w, 16)
            sp.wait_ge(k_pool, 1)
            for h in range(2):
                at_ = slice(h * DHEAD, (h + 1) * DHEAD)
                for l in range(2):
                    sp.dma_start(gw[at_, l, at_], gnn_w[l]).then_inc(w_small, 16)
                    sp.dma_start(gb[at_, l:l + 1], gnn_b[l:l + 1, :].rearrange("o d -> d o")).then_inc(w_small, 16)
                sp.dma_start(linT[at_, at_], lin_wT).then_inc(w_small, 16)
                sp.dma_start(lb[at_, :], lin_b).then_inc(w_small, 16)
            sp.dma_start(x_all[:, TILES:, :], xv[:, TILES:, :]).then_inc(w_x, 16)

            sp.wait_ge(k_pool, 3)
            for r in range(0, SLOT_ROWS, CLEAR * P):
                sp.dma_start(slots[r:r + CLEAR * P, :].rearrange("(p r) d -> p (r d)", p=P),
                             zero[:, :]).then_inc(w_clear, 16)

            sp.wait_ge(k_dve, 5)
            for c, (at_, n) in enumerate(CHUNKS):
                sp.dma_start(dn[0:n, :, c, :], downT[:, at_:at_ + n, :].rearrange("e p d -> p e d")).then_inc(w_dn, 16)
            for e in range(EXPERTS):
                if e >= 2:
                    sp.wait_ge(k_gu, 2 * (e - 1))
                sp.dma_start(raw_gu[:, e % 2, :], guT[e]).then_inc(w_gu[e % 2], 16)

            def rows_of(regs, g):
                if isinstance(g, int) and not 0 <= g < GROUPS:
                    return None
                sp.load(regs, step_row[0:1, bass.ds(g * UNROLL, UNROLL)])
                return [sp.snap(r, min_val=0, max_val=SLOT_ROWS - P) for r in regs]

            def load(g, i, row):
                if live(g, i - UNROLL):
                    s_tz.wait(sp, step(g, i - UNROLL), 1)
                sp.dma_start(zin[:, i, :], slots[bass.ds(row, P), :]).then_inc(w_zin[i].sem, 16)

            def store(g, i, row):
                d_zout.wait(sp, step(g, i), 1)
                sp.dma_start(slots[bass.ds(row, P), :], zout[:, i, :]).then_inc(w_zout[i].sem, 16)

            def sorted_group(g):
                into, back = rows_of(load_reg, g), rows_of(store_reg, g - LATE)
                for i in range(UNROLL):
                    if into is not None:
                        load(g, i, into[i])
                    if back is not None:
                        store(g - LATE, i, back[i])

            load_reg = [sp.alloc_register(f"load_row{i}") for i in range(UNROLL)]
            store_reg = [sp.alloc_register(f"store_row{i}") for i in range(UNROLL)]
            sp.wait_ge(d_tab, TABLES)
            for g in range(2):
                sorted_group(g)
            with sp.Fori(2, GROUPS) as g:
                sorted_group(g)
            sorted_group(GROUPS)
            sorted_group(GROUPS + 1)

            ov = out.rearrange("(t p) d -> p t d", p=P)
            for t in range(0, ROOM, BT):
                sp.wait_ge(d_fin, 2 * (t + BT))
                sp.dma_start(ov[:, t:t + BT, :], x_all[:, t:t + BT, :]).then_inc(w_out, 16)
            sp.wait_ge(d_acc, EXPERTS)
            sp.dma_start(ov[:, ROOM:, :], acc[:, :, :]).then_inc(w_out, 16)
            sp.wait_ge(w_out, 16 * (ROOM // BT + 1))

        @block.gpsimd
        def _(pool):
            nc.gpsimd.memset(gw[:, :, :], 0.0)
            nc.gpsimd.memset(linT[:, :], 0.0).then_inc(k_pool, 1)
            nc.gpsimd.memset(half[:, :], -0.5)
            nc.gpsimd.memset(zero[:, :], 0.0)
            nc.gpsimd.memset(before_f[:, :], 1.0)
            nc.gpsimd.memset(upto[:, :, :], 1.0)
            nc.gpsimd.memset(ones_bf[:, :], 1.0)
            nc.gpsimd.memset(eq_bf[:, :, :], 0.0)
            nc.gpsimd.memset(ident[:, :], 0.0)
            nc.gpsimd.memset(idw[:, :], 0.0)
            nc.gpsimd.memset(maskf[:, :], 0.0)
            nc.gpsimd.memset(kT[:, :, :, :], 0.0).then_inc(k_pool, 1)
            pool.wait_ge(k_pool, 2)
            for m in (ident[:, :], idw[:, P:2 * P]):
                nc.gpsimd.affine_select(out=m, in_=m, compare_op=ALU.not_equal, fill=1.0,
                                        base=0, pattern=[[-1, P]], channel_multiplier=1)
            nc.gpsimd.affine_select(out=maskf[:, :], in_=maskf[:, :], compare_op=ALU.is_ge, fill=MASKED,
                                    base=0, pattern=[[-1, P]], channel_multiplier=1)
            nc.gpsimd.affine_select(out=before_f[:, :], in_=before_f[:, :], compare_op=ALU.is_gt, fill=0.0,
                                    base=0, pattern=[[1, P]], channel_multiplier=-1)
            nc.gpsimd.affine_select(out=upto[:, :, :], in_=upto[:, :, :], compare_op=ALU.is_ge, fill=0.0,
                                    base=0, pattern=[[1, EXPERTS], [-1, EXPERTS]], channel_multiplier=0)
            for o, by in ((iot, 1), (first_row, ROOM * P), (next_row, ROOM * P), (tile_from, P), (step_no, 1)):
                done = nc.gpsimd.iota(o[:, :], pattern=[[by, o.shape[1]]], base=0, channel_multiplier=0,
                                      allow_small_or_imprecise_dtypes=True)
            done.then_inc(k_pool, 1)

            def deviation(b, step, d_step):
                d_ln.wait(pool, b, d_step)
                nc.gpsimd.tensor_tensor(rstd[:, :], ve[:, :], half[:, 0:TILES], ALU.pow).then_inc(p_ln.sem, 1)

            def graph(b, n):
                s = n % 3
                d_w.wait(pool, b, n + 1)
                nc.gpsimd.tensor_tensor(ea[:, s], ea[:, s],
                                        wgt[:, s, 0:2].unsqueeze(2).to_broadcast([P, 2, P]), ALU.mult)
                nc.gpsimd.tensor_tensor(eb[:, s], eb[:, s],
                                        wgt[:, s, 2:4].unsqueeze(2).to_broadcast([P, 2, 2 * P]),
                                        ALU.mult).then_inc(p_g.sem, 1)
                nc.gpsimd.tensor_tensor(deg[:, s], den[:, s, :].unsqueeze(2).to_broadcast([P, 4, DHEAD]),
                                        rs[:, s, :].unsqueeze(2).to_broadcast([P, 4, DHEAD]),
                                        ALU.mult).then_inc(p_deg.sem, 1)

            def token_power(p, i):
                d_st.wait(pool, p, POWERS[i])
                nc.gpsimd.tensor_tensor(rs4[:, :], ve4[:, :], half[:, :], ALU.pow).then_inc(p_st.sem, 1)

            def scatter(p, c):
                nc.gpsimd.indirect_dma_start(slots, bass.IndirectOffsetOnAxis(ap=row_now[:, c:c + 1], axis=0),
                                             z4[:, c % TILES, :], None).then_inc(z_free.sem, 16)

            def phase2(b, before, after):
                if before is not None:
                    token_power(before, 0)
                if after is not None:
                    deviation(after, 0, 3)
                if before is not None:
                    token_power(before, 1)
                if after is not None:
                    deviation(after, 1, 7)
                if before is not None:
                    token_power(before, 2)

            def phase1(b, before):
                for n in range(PAIRS):
                    if before is not None and n == PAIRS - 3:
                        d_pl.wait(pool, before, 6)
                    graph(b, n)
                    if before is not None and n == PAIRS - 3:
                        scatter(before, 0)
                    if before is not None and n >= PAIRS - 3:
                        scatter(before, n - (PAIRS - 4))
                if before is not None:
                    z_free.wait(pool, before, z_free.per)

            deviation(0, 0, 3)
            deviation(0, 1, 7)
            pool.wait_ge(k_dve, 5)
            nc.gpsimd.memset(dn[CHUNKS[-1][1]:P, :, NC - 1, :], 0.0).then_inc(k_pool, 1)
            pool.wait_ge(k_pool, 4)
            phase1(0, None)
            phase2(0, None, 1)
            phase1(1, None)
            pool.wait_ge(w_clear, 16 * (SLOT_ROWS // (CLEAR * P)))
            with pool.Fori(1, BATCHES - 1) as b:
                phase2(b, b - 1, b + 1)
                phase1(b + 1, b - 1)
            phase2(BATCHES - 1, BATCHES - 2, None)
            for i in range(3):
                token_power(BATCHES - 1, i)

            for s in range(UNROLL):
                w_zout[s].wait(pool, GROUPS, 0)
            for q in range(ROOM):
                if q >= UNROLL:
                    pool.wait_ge(d_fin, 2 * (q - UNROLL + 1))
                for r in range(CHOICES):
                    nc.gpsimd.indirect_dma_start(
                        got[:, q % UNROLL, r, :], None, slots,
                        bass.IndirectOffsetOnAxis(ap=row_all[:, q // TILES, r * TILES + q % TILES:][:, 0:1],
                                                  axis=0)).then_inc(w_got[q % UNROLL], 16)

        @block.tensor
        def _(pe):
            def product(o, st, mo, first, last, **more):
                nc_mm = nc.tensor.matmul
                return nc_mm(o, st, mo, start=first, stop=last, **more)

            def product3(o, st_hi, st_lo, mo_hi, mo_lo, first=True, last=True, **more):
                product(o, st_hi, mo_lo, first, False, **more)
                product(o, st_lo, mo_hi, False, False, **more)
                return product(o, st_hi, mo_hi, False, last, **more)

            def prepare_weights():
                pe.wait_ge(k_pool, 3)
                pe.wait_ge(w_w, 5 * 16)
                pe.wait_ge(w_small, SMALL_ALL)
                for g in range(PAIRS):
                    mm = product(bank[2 + g // 4][:, (g % 4) * P:(g % 4 + 1) * P], linT[:, :], wo_sb[:, g, :], True, True)
                mm.then_inc(k_pe, 1)
                for g in range(PAIRS):
                    mm = product(bank[4][:, 0:P], wvt[:, g, :], wo_sb[:, g, :], g == 0, g == PAIRS - 1)
                for g in range(PAIRS):
                    mm = product(bank[5][:, 0:1], wo_sb[:, g, :], lb[:, :], g == 0, g == PAIRS - 1)
                mm.then_inc(k_pe, 1)

            def x_transposed(b):
                d_ln.wait(pe, b, 8)
                for t in range(TILES):
                    mm = nc.tensor.transpose(bank[6][:, xt(t)], xn[:, t, :], ident[:, :])
                mm.then_inc(s_xt.sem, 1)

            def values(b, c, earlier):
                t, h = c // 2, c % 2
                if earlier is not None:
                    (d_z1, a_g1, a_g1, d_z2)[c].wait(pe, earlier, (PAIRS, PAIRS - 1, PAIRS, PAIRS - 1)[c])
                cols = slice(h * 512, (h + 1) * 512)
                product3(bank[1 + c][:, :], xt_hi[:, xt(t)], xt_lo[:, xt(t)],
                         v_hi[:, cols], v_lo[:, cols]).then_inc(s_v.sem, 1)

            def queries_keys(b, n):
                if n == 0:
                    a_xt.wait(pe, b, 1)
                    d_xt.wait(pe, b, 1)
                else:
                    a_qk.wait(pe, b, n)
                cols = slice(n * P, (n + 1) * P)
                product3(bank[0][:, 0:TOKENS], w_hi[:, 0, cols], w_lo[:, 0, cols], xt_hi[:, :], xt_lo[:, :])
                product3(bank[0][:, TOKENS:], w_hi[:, 1, cols], w_lo[:, 1, cols],
                         xt_hi[:, :], xt_lo[:, :]).then_inc(s_qk.sem, 1)

            def scores(b, n):
                a_qk.wait(pe, b, n + 1)
                if n == 0:
                    a_v.wait(pe, b, 2)
                else:
                    a_exp.wait(pe, b, 2 * n - 1)
                q, k = qT[:, n % 2], kT[:, n % 2]
                product(bank[1][:, 0:2 * P], ident_bf[:, :], mask[:, :, :], True, False)
                product(bank[1][:, 0:2 * P], q[:, xt(0)], k[:, :, xt(0)], False, True).then_inc(s_s.sem, 1)
                if n >= 1:
                    a_exp.wait(pe, b, 2 * n)
                sb1 = bank[2][:, :].rearrange("p (h j) -> p h j", h=2)
                product(sb1[:, :, xt(1)], ident_bf[:, :], mask[:, :, :], True, False, skip_group_check=True)
                product(bank[2][:, :], q[:, xt(1)], k[:, :, :], False, True,
                        skip_group_check=True).then_inc(s_s.sem, 1)

            def transposes(b, n):
                s = n % 3
                p_g.wait(pe, b, n + 1)
                if n >= 1:
                    a_gt.wait(pe, b, n)
                else:
                    a_v.wait(pe, b, 4)
                for a in range(2):
                    nc.tensor.transpose(bank[3][:, a * TOKENS:a * TOKENS + P], ea[:, s, a, :], ident[:, :])
                    nc.tensor.transpose(bank[3][:, a * TOKENS + P:(a + 1) * TOKENS], eb[:, s, a, 0:P], ident[:, :])
                for a in range(2):
                    mm = nc.tensor.transpose(bank[4][:, a * P:(a + 1) * P], eb[:, s, a, P:], ident[:, :])
                mm.then_inc(s_t.sem, 1)

            def mixed(o, left, n):
                for tile, moving, cols in ((0, gt0, slice(0, TOKENS)), (1, gt1, slice(P, TOKENS))):
                    for a in range(2):
                        rows = slice(a * DHEAD, (a + 1) * DHEAD)
                        mm = product(o[rows, cols], left(tile, a), moving[:, n, a, :], tile == 0,
                                     tile == 1, skip_group_check=True)
                return mm

            def differences(b, n):
                a_gt.wait(pe, b, n + 1)
                if n == 0:
                    a_v.wait(pe, b, 4)
                else:
                    a_d.wait(pe, b, n)
                mixed(bank[5][:, 0:TOKENS], lambda t, a: vnat[:, t, n * P + a * DHEAD:n * P + (a + 1) * DHEAD], n)
                for t in range(TILES):
                    mm = nc.tensor.transpose(bank[5][:, TOKENS + t * P:TOKENS + (t + 1) * P],
                                             vnat[:, t, n * P:(n + 1) * P], ident[:, :])
                mm.then_inc(s_d.sem, 1)

            def degrees(b, n):
                p_deg.wait(pe, b, n + 1)
                if n >= 1:
                    d_a.wait(pe, b, n)
                for t in range(TILES):
                    mm = nc.tensor.transpose(
                        bank[6][:, xt(t)],
                        deg[:, n % 3, 2 * t:2 * t + 2, :].rearrange("p a c -> p (a c)"), ident[:, :])
                mm.then_inc(s_deg.sem, 1)

            def output_natural(b):
                d_yT.wait(pe, b, 1)
                for t in range(TILES):
                    mm = nc.tensor.transpose(bank[7][:, xt(t)], yT[:, xt(t)], ident[:, :])
                mm.then_inc(s_yn.sem, 1)

            def layer1(b, n):
                a_d.wait(pe, b, n + 1)
                if n >= 2:
                    d_z1.wait(pe, b, n - 1)
                product(bank[n % 2][:, 0:TOKENS], gw[:, 0, :], gvT[:, n, :], True, True).then_inc(s_f1.sem, 1)

            def layer2_in(b, n):
                a_f1.wait(pe, b, n + 1)
                if n >= 2:
                    a_g1.wait(pe, b, n - 1)
                for t in range(TILES):
                    mm = product(bank[2 + n % 2][:, xt(t)], f1T[:, n % 4, xt(t)], gw[:, 1, :], True, True)
                mm.then_inc(s_g1.sem, 1)

            def layer2(b, n):
                a_g1.wait(pe, b, n + 1)
                if n >= 2:
                    d_z2.wait(pe, b, n - 1)
                mixed(bank[4 + n % 2][:, 0:TOKENS],
                      lambda t, a: g1[:, n % 2, t, a * DHEAD:(a + 1) * DHEAD], n).then_inc(s_h2.sem, 1)

            def output_start(b, before):
                if before is not None:
                    d_y.wait(pe, before, 1)
                product3(bank[7][:, 0:TOKENS], cy_hi[:, :], cy_lo[:, :], xt_hi[:, :], xt_lo[:, :], last=False)

            def output_graph(b, n):
                a_f2.wait(pe, b, n + 1)
                product(bank[7][:, 0:TOKENS], lwo[:, n, :], f2T[:, n % 2, :], False, False)

            def output_attended(b, pairs):
                if pairs[0] == 0:
                    d_a.wait(pe, b, PAIRS)
                for n in pairs:
                    mm = product(bank[7][:, 0:TOKENS], wo_sb[:, n, :], aT[:, n, :], False, n == PAIRS - 1)
                if n == PAIRS - 1:
                    mm.then_inc(s_y.sem, 1)

            HALVES = (range(0, PAIRS // 2), range(PAIRS // 2, PAIRS))

            def phase1(b, before, tokens_of=None):
                for n in range(PAIRS + 2):
                    if n == PAIRS + 1:
                        layer1(b, 1)
                        if tokens_of is not None:
                            d_pl.wait(pe, tokens_of, 3)
                        output_start(b, before)
                    if n >= 2:
                        transposes(b, n - 2)
                    if n + 1 < PAIRS:
                        queries_keys(b, n + 1)
                    if n < PAIRS:
                        scores(b, n)
                    if tokens_of is not None:
                        if n == 1:
                            logits(tokens_of, bank[6])
                        if n == 2:
                            d_ch.wait(pe, tokens_of, 1)
                        if n == 4:
                            d_y.wait(pe, before, 1)
                            places(tokens_of)
                    if n == 0 and before is not None:
                        output_graph(before, PAIRS - 1)
                    if n <= 1 and before is not None:
                        output_attended(before, HALVES[n])
                    if n == PAIRS:
                        layer1(b, 0)
                    if n == PAIRS + 1:
                        layer2_in(b, 0)
                    if n >= 2:
                        differences(b, n - 2)
                        degrees(b, n - 2)
                    if n == 2 and before is not None:
                        output_natural(before)

            def phase2(b, before, after):
                for n in range(2, PAIRS + 2):
                    if n < PAIRS:
                        layer1(b, n)
                    if n - 1 < PAIRS:
                        layer2_in(b, n - 1)
                    layer2(b, n - 2)
                    if n >= 3:
                        output_graph(b, n - 3)
                    if after is not None:
                        if n == 7:
                            d_a.wait(pe, b, PAIRS)
                            x_transposed(after)
                        if n == 8:
                            d_z1.wait(pe, b, PAIRS - 1)
                            queries_keys(after, 0)
                        if n == 9:
                            for c in range(4):
                                values(after, c, b)
                    if before is not None and n == 9:
                        if after is not None:
                            d_xt.wait(pe, after, 1)
                        else:
                            d_a.wait(pe, b, PAIRS)
                        tokens_transposed(before, bank[6])

            def tokens_transposed(p, o):
                d_st.wait(pe, p, NORMED)
                for t in range(TILES):
                    mm = nc.tensor.transpose(o[:, xt(t)], z4[:, t, :], ident[:, :])
                mm.then_inc(s_zt.sem, 1)

            def logits(p, o):
                a_zt.wait(pe, p, 1)
                for t in range(TILES):
                    mm = product(o[:, t * EXPERTS:(t + 1) * EXPERTS], zT[:, xt(t)], rtT[:, :], True, True)
                mm.then_inc(s_lg.sem, 1)

            def places(p):
                d_ch.wait(pe, p, ONE_HOT)
                o = bank[7][:, PLACES].rearrange("p (c e) -> p c e", e=EXPERTS)
                product(o, before_bf[:, :], eq_bf[:, :, :], True, False, skip_group_check=True)
                for c in range(SIDE):
                    mm = product(o[:, c + 1:, :], ones_bf[:, :],
                                 eq_bf[:, c:c + 1, :].to_broadcast([P, SIDE - c, EXPERTS]), False, c == SIDE - 1,
                                 skip_group_check=True)
                mm.then_inc(s_pre.sem, 1)

            expert_reg = [pe.alloc_register(f"expert{i}") for i in range(2 * UNROLL)]

            def load_experts(g):
                first = min(g, 1) if isinstance(g, int) else 1
                n = UNROLL * (1 + first)
                pe.load(expert_reg[:n], step_expert[0:1, bass.ds((g - first) * UNROLL, n)])
                e = [pe.snap(r, min_val=0, max_val=EXPERTS - 1) for r in expert_reg[:n]]
                return {i - first * UNROLL: v for i, v in enumerate(e)}

            def slots_transposed(g, i):
                if not live(g, i):
                    return
                q, s = turn(g, i)
                w_zin[s].wait(pe, q, 16)
                nc.tensor.transpose(bank[4][:, 0:P], zin[:, s, :], ident[:, :]).then_inc(s_tz.sem, 1)

            def sorted_gate_up(g, i, expert):
                if not live(g, i):
                    return
                j = step(g, i)
                e = expert[i]
                d_zlo.wait(pe, j, 1)
                if live(g, i - 2):
                    d_hid.wait(pe, step(g, i - 2), 1)
                def half_of(w, part):
                    return w[:, bass.ds(e, 1), part * HID:(part + 1) * HID].rearrange("p o h -> p (o h)")
                for part in range(2):
                    mm = product3(bank[2 * part + i % 2][:, 0:HID], sz_hi[:, i % 2, :], sz_lo[:, i % 2, :],
                                  half_of(gu_hi, part), half_of(gu_lo, part))
                    if part == 0:
                        mm.then_inc(s_gu.sem, 1)
                mm.then_inc(s_gu.sem, 1)

            def hidden_transposed(g, i):
                if not live(g, i):
                    return
                d_hid.wait(pe, step(g, i), 1)
                if live(g, i - 2):
                    a_ht.wait(pe, step(g, i - 2), 1)
                for c in range(NC):
                    mm = nc.tensor.transpose(bank[5 + i % 2][:, xt(c)], shid[:, i % 2, xt(c)], ident[:, :])
                mm.then_inc(s_ht.sem, 1)

            def sorted_down(g, i, expert):
                if not live(g, i):
                    return
                e = expert[i]
                a_ht.wait(pe, step(g, i), 1)
                if live(g, i - 1):
                    d_zout.wait(pe, step(g, i - 1), 1)
                for c in range(NC):
                    mm = product(bank[7][:, 0:DIM], shT[:, i % 2, c, :],
                                 dn[:, bass.ds(e, 1), c, :].rearrange("p o d -> p (o d)"), c == 0, c == NC - 1)
                mm.then_inc(s_down.sem, 1)

            def sorted_group(g):
                expert = load_experts(g)
                for i in range(UNROLL):
                    sorted_gate_up(g, i, expert)
                    if live(g, i + 1):
                        d_zlo.wait(pe, step(g, i + 1), 1)
                    kept_tokens(g, i)
                    slots_transposed(g, i + 2)
                    if isinstance(g, int) and g == 0 and i == 0:
                        output_natural(BATCHES - 1)
                        d_y.wait(pe, BATCHES - 1, 1)
                    sorted_down(g, i - 2, expert)
                    hidden_transposed(g, i - 1)
                return expert

            def kept_tokens(g, i):
                if isinstance(g, int):
                    j = step(g, i)
                    if j == 1:
                        logits(BATCHES - 2, bank[4])
                        d_ch.wait(pe, BATCHES - 2, 1)
                    if j == KEPT_Z:
                        tokens_transposed(BATCHES - 1, bank[4])
                        a_zt.wait(pe, BATCHES - 1, 1)
                    if j == KEPT_Z + 1:
                        logits(BATCHES - 1, bank[4])
                        d_ch.wait(pe, BATCHES - 1, 1)

            def sorted_stage():
                d_z1.wait(pe, BATCHES - 1, PAIRS)
                a_g1.wait(pe, BATCHES - 1, PAIRS)
                d_z2.wait(pe, BATCHES - 1, PAIRS)
                pe.wait_ge(k_gu, 2 * EXPERTS)
                pe.wait_ge(w_dn, 16 * NC)
                for g in range(2):
                    sorted_group(g)
                with pe.Fori(2, GROUPS - 1) as g:
                    sorted_group(g)
                expert = {i - UNROLL: e for i, e in sorted_group(GROUPS - 1).items()}
                sorted_down(GROUPS, -2, expert)
                hidden_transposed(GROUPS, -1)
                sorted_down(GROUPS, -1, expert)

            def gate_up(i):
                e, c = i // NC, i % NC
                at_, n = CHUNKS[c]
                for part, o, done in ((0, bank[i % 2], s_gt), (1, bank[2 + i % 2], s_up)):
                    cols = slice(part * HID + at_, part * HID + at_ + n)
                    if part == 0 and i >= 2:
                        pe.wait_ge(a_sg, i - 1)
                    if part == 1 and i >= 2:
                        pe.wait_ge(d_h, i - 1)
                    product3(o[0:n, :], gu_hi[:, e, cols], gu_lo[:, e, cols],
                             zt[:, 0, :], zt[:, 1, :]).then_inc(done, 1)

            def down(e):
                pe.wait_ge(d_h, (e + 1) * NC)
                if e >= 2:
                    pe.wait_ge(d_acc, e - 1)
                for t in range(BT):
                    for c, (_, n) in enumerate(CHUNKS):
                        mm = product(bank[4 + e % 2][:, xt(t)], hT[0:n, e % 2, c, xt(t)], dn[0:n, e, c, :],
                                     c == 0, c == NC - 1)
                mm.then_inc(s_dn, 1)

            def every_expert():
                pe.wait_ge(d_zt, 2 * KEPT)
                d_hid.wait(pe, STEPS, 0)
                for i in range(EXPERTS * NC):
                    gate_up(i)
                    if i == 0:
                        a_ht.wait(pe, STEPS, 0)
                        pe.wait_ge(d_comb, KEPT)
                    if i % NC == 0 and i > 0:
                        down(i // NC - 1)
                down(EXPERTS - 1)

            prepare_weights()
            x_transposed(0)
            pe.wait_ge(k_dve, 5)
            queries_keys(0, 0)
            for c in range(4):
                values(0, c, None)
            phase1(0, None)
            phase2(0, None, 1)
            phase1(1, 0)
            with pe.Fori(1, BATCHES - 1) as b:
                phase2(b, b - 1, b + 1)
                phase1(b + 1, b, b - 1)
            phase2(BATCHES - 1, BATCHES - 2, None)
            output_graph(BATCHES - 1, PAIRS - 1)
            for half_ in HALVES:
                output_attended(BATCHES - 1, half_)

            slots_transposed(0, 0)
            d_zlo.wait(pe, 0, 1)
            slots_transposed(0, 1)
            sorted_stage()
            every_expert()

        @block.scalar
        def _(act):
            def copy(o, i, **more):
                return nc.scalar.activation(o, i, ACT.Copy, **more)

            def prepare_weights():
                act.wait_ge(k_pe, 1)
                copy(lwo[:, 0:4, :], bank[2][:, :].rearrange("p (g n) -> p g n", g=4))
                copy(lwo[:, 4:8, :], bank[3][:, :].rearrange("p (g n) -> p g n", g=4))
                act.wait_ge(k_pe, 2)
                copy(yb[:, :], bank[5][:, 0:1]).then_inc(k_act, 1)

            def x_high(b, earlier):
                s_xt.wait(act, b, 1)
                if earlier is not None:
                    s_f1.wait(act, earlier, PAIRS)
                copy(xt_hi[:, :], bank[6][:, 0:TOKENS], scale=gin[:, :]).then_inc(a_xt.sem, 1)

            def values(b, c):
                s_v.wait(act, b, c + 1)
                t, h = c // 2, c % 2
                copy(vnat[:, t, h * 512:(h + 1) * 512], bank[1 + c][:, :]).then_inc(a_v.sem, 1)

            def queries_keys(b, n):
                s_qk.wait(act, b, n + 1)
                copy(qT[:, n % 2, :], bank[0][:, 0:TOKENS])
                for a in range(2):
                    rows = slice(a * DHEAD, (a + 1) * DHEAD)
                    done = copy(kT[rows, n % 2, a, :], bank[0][rows, TOKENS:], scale=SCALE)
                done.then_inc(a_qk.sem, 1)

            def exps(b, n, t):
                d_max.wait(act, b, 2 * n + 1 + t)
                s, width = n % 3, (t + 1) * P
                e = eb if t else ea
                for a in range(2):
                    i = 2 * t + a
                    done = nc.scalar.activation(e[:, s, a, :], bank[1 + t][:, a * width:(a + 1) * width], ACT.Exp,
                                                bias=nmax[:, s, i:i + 1], accum_out=ssum[:, s, i:i + 1])
                done.then_inc(a_exp.sem, 1)

            def graph(b, n):
                s_t.wait(act, b, n + 1)
                copy(gt0[:, n, :, :], bank[3][:, :].rearrange("p (a i) -> p a i", a=2))
                copy(gt1[:, n, :, :], bank[4][:, 0:2 * P].rearrange("p (a i) -> p a i", a=2)).then_inc(a_gt.sem, 1)

            def differences(b, n):
                s_d.wait(act, b, n + 1)
                copy(gvT[:, n, :], bank[5][:, 0:TOKENS])
                copy(vT[:, n, :], bank[5][:, TOKENS:]).then_inc(a_d.sem, 1)

            def gelu1(b, n):
                d_z1.wait(act, b, n + 1)
                nc.scalar.activation(f1T[:, n % 4, :], z1[:, n % 2, :], ACT.Gelu,
                                     bias=gb[:, 0:1]).then_inc(a_f1.sem, 1)

            def layer2_in(b, n):
                s_g1.wait(act, b, n + 1)
                copy(g1[:, n % 2, :, :],
                     bank[2 + n % 2][:, 0:TOKENS].rearrange("p (t d) -> p t d", t=TILES)).then_inc(a_g1.sem, 1)

            def gelu2(b, n):
                d_z2.wait(act, b, n + 1)
                nc.scalar.activation(f2T[:, n % 2, :], z2[:, n % 2, :], ACT.Gelu,
                                     bias=gb[:, 1:2]).then_inc(a_f2.sem, 1)

            def phase1(b, tokens_of=None):
                for n in range(PAIRS + 2):
                    if n >= 2:
                        graph(b, n - 2)
                    if n + 1 < PAIRS:
                        queries_keys(b, n + 1)
                    if n < PAIRS:
                        exps(b, n, 0)
                        exps(b, n, 1)
                    if n >= PAIRS:
                        gelu1(b, n - PAIRS)
                    if n >= 2:
                        differences(b, n - 2)
                    if tokens_of is not None and n == 2:
                        shares_ratio(tokens_of)

            def phase2(b, before, after):
                layer2_in(b, 0)
                for n in range(2, PAIRS + 2):
                    if n < PAIRS:
                        gelu1(b, n)
                    if n - 1 < PAIRS:
                        layer2_in(b, n - 1)
                    if n == 8 and after is not None:
                        x_high(after, b)
                    if after is not None and n == 9:
                        queries_keys(after, 0)
                    gelu2(b, n - 2)
                    if after is not None and n == 9:
                        for c in range(4):
                            values(after, c)
                    if before is not None and n == 9:
                        tokens_transposed(before, bank[6])

            def tokens_transposed(p, o):
                s_zt.wait(act, p, 1)
                copy(zT[:, :], o[:, 0:TOKENS], scale=normw[:, :]).then_inc(a_zt.sem, 1)

            def shares_ratio(p):
                d_ch.wait(act, p, GAP)
                nc.scalar.activation(ratio[:, :], gap[:, :], ACT.Exp, scale=-1.0).then_inc(a_ratio.sem, 1)

            def slots_high(g, i):
                if not live(g, i):
                    return
                s_tz.wait(act, step(g, i), 1)
                if live(g, i - 2):
                    s_gu.wait(act, 2 * step(g, i - 2), 2)
                copy(sz_hi[:, i % 2, :], bank[4][:, 0:P], scale=normw[:, :]).then_inc(a_zh.sem, 1)

            def silu(g, i):
                if not live(g, i):
                    return
                s_gu.wait(act, 2 * step(g, i), 1)
                if live(g, i - 2):
                    d_hid.wait(act, step(g, i - 2), 1)
                nc.scalar.activation(ssg[:, i % 2, :], bank[i % 2][:, 0:HID], ACT.Silu).then_inc(a_silu.sem, 1)

            def hidden_transposed(g, i):
                if not live(g, i):
                    return
                s_ht.wait(act, step(g, i), 1)
                if live(g, i - 2):
                    s_down.wait(act, step(g, i - 2), 1)
                copy(shT[:, i % 2, :, :],
                     bank[5 + i % 2][:, 0:NC * P].rearrange("p (c n) -> p c n", c=NC)).then_inc(a_ht.sem, 1)

            def sorted_group(g):
                for i in range(UNROLL):
                    silu(g, i)
                    if isinstance(g, int) and step(g, i) == KEPT_Z:
                        tokens_transposed(BATCHES - 1, bank[4])
                    slots_high(g, i + 2)
                    hidden_transposed(g, i - 1)
                    if isinstance(g, int) and step(g, i) == 4:
                        shares_ratio(BATCHES - 2)

            def sorted_stage():
                slots_high(0, 0)
                slots_high(0, 1)
                for g in range(2):
                    sorted_group(g)
                with act.Fori(2, GROUPS - 1) as g:
                    sorted_group(g)
                sorted_group(GROUPS - 1)
                hidden_transposed(GROUPS, -1)

            def every_expert():
                for i in range(EXPERTS * NC):
                    n = CHUNKS[i % NC][1]
                    act.wait_ge(s_gt, i + 1)
                    if i >= 2:
                        act.wait_ge(d_h, i - 1)
                    nc.scalar.activation(sg[0:n, i % 2, :], bank[i % 2][0:n, :], ACT.Silu).then_inc(a_sg, 1)

            act.wait_ge(w_small, SMALL_ALL)
            act.wait_ge(k_pool, 2)
            prepare_weights()
            x_high(0, None)
            queries_keys(0, 0)
            for c in range(4):
                values(0, c)
            phase1(0)
            phase2(0, None, 1)
            phase1(1)
            with act.Fori(1, BATCHES - 1) as b:
                phase2(b, b - 1, b + 1)
                phase1(b + 1, b - 1)
            phase2(BATCHES - 1, BATCHES - 2, None)
            sorted_stage()
            shares_ratio(BATCHES - 1)
            every_expert()

        @block.vector
        def _(dve):
            V = nc.vector

            def prepare_weights():
                dve.wait_ge(k_pool, 3)
                V.tensor_copy(ident_bf[:, :], ident[:, :])
                V.tensor_copy(before_bf[:, :], before_f[:, :])
                for a in range(2):
                    V.tensor_copy(mask[:, a, :], maskf[:, :])
                dve.wait_ge(w_w, 5 * 16)
                V.tensor_copy(v_hi[:, :], raw[:, 2, :])
                for n in range(2):
                    done = V.tensor_copy(w_hi[:, n, :], raw[:, n, :])
                done.then_inc(k_dve, 1)
                dve.wait_ge(k_dve, 1)
                V.tensor_tensor(v_lo[:, :], raw[:, 2, :], v_hi[:, :].bitcast(f32), ALU.subtract)
                for n in range(2):
                    done = V.tensor_tensor(w_lo[:, n, :], raw[:, n, :], w_hi[:, n, :].bitcast(f32), ALU.subtract)
                done.then_inc(k_dve, 1)
                dve.wait_ge(k_pe, 2)
                V.tensor_copy(cy_hi[:, :], bank[4][:, 0:P]).then_inc(k_dve, 1)
                dve.wait_ge(k_dve, 3)
                V.tensor_tensor(cy_lo[:, :], bank[4][:, 0:P], cy_hi[:, :].bitcast(f32),
                                ALU.subtract).then_inc(k_dve, 1)
                dve.wait_ge(k_act, 1)
                dve.wait_ge(w_small, SMALL_ALL)
                dve.wait_ge(k_dve, 4)
                V.tensor_scalar(alph[:, :], alph[:, :], -0.5, 2.0, ALU.max, ALU.min).then_inc(k_dve, 1)

            def wait_ahead(signal, turn, k):
                signal.wait(dve, turn, k)
                V.memset(hold[:, :], 0.0)

            def stats(b, src, step):
                for t in range(TILES):
                    done = V.bn_stats(stat[:, t, :], src(t))
                done.then_inc(d_ln.sem, 1)

            def aggregate(b, step):
                wait_ahead(d_ln, b, step)
                for t in range(TILES):
                    done = V.bn_aggr(mv_[:, t, :], stat[:, t, :])
                done.then_inc(d_ln.sem, 1)
                d_ln.wait(dve, b, step + 1)
                V.tensor_scalar(ve[:, :], mv_[:, :, 1], EPS_LN, None, ALU.add).then_inc(d_ln.sem, 1)

            def normalise(b, step, power, o, src):
                p_ln.wait(dve, b, power)
                for t in range(TILES):
                    done = V.tensor_scalar(o[:, t, :], src(t), mv_[:, t, 0:1], rstd[:, t:t + 1],
                                           ALU.subtract, ALU.mult)
                done.then_inc(d_ln.sem, 1)

            def x_tile(b):
                return lambda t: x_all[:, bass.ds(b * TILES + t, 1), :].rearrange("p o d -> p (o d)")

            def norm_step(b, i):
                if i == 0:
                    stats(b, x_tile(b), 0)
                if i == 1:
                    aggregate(b, 1)
                if i == 2:
                    normalise(b, 3, 1, xh, x_tile(b))
                if i == 3:
                    wait_ahead(d_ln, b, 4)
                    stats(b, lambda t: xh[:, t, :], 4)
                if i == 4:
                    aggregate(b, 5)
                if i == 5:
                    normalise(b, 7, 2, xn, lambda t: xh[:, t, :])

            def x_low(b):
                a_xt.wait(dve, b, 1)
                V.scalar_tensor_tensor(xt_lo[:, :], bank[6][:, 0:TOKENS], gin[:, :],
                                       xt_hi[:, :].bitcast(f32), ALU.mult, ALU.subtract).then_inc(d_xt.sem, 1)

            def maxima(b, n, t):
                s_s.wait(dve, b, 2 * n + 1 + t)
                width = (t + 1) * P
                V.tensor_reduce(nmax[:, n % 3, 2 * t:2 * t + 2],
                                bank[1 + t][:, 0:2 * width].rearrange("p (a j) -> p a j", a=2), X, ALU.max,
                                negate=True).then_inc(d_max.sem, 1)

            def adjacency(b, n):
                s = n % 3
                a_exp.wait(dve, b, 2 * n + 2)
                V.reciprocal(rs[:, s, :], ssum[:, s, :])
                for a in range(2):
                    V.scalar_tensor_tensor(ea[:, s, a, :], ident[:, :], ssum[:, s, a:a + 1], ea[:, s, a, :],
                                           ALU.mult, ALU.max, accum_out=den[:, s, a:a + 1])
                for a in range(2):
                    done = V.scalar_tensor_tensor(eb[:, s, a, :], idw[:, :], ssum[:, s, 2 + a:3 + a],
                                                  eb[:, s, a, :], ALU.mult, ALU.max,
                                                  accum_out=den[:, s, 2 + a:3 + a])
                done.then_inc(d_e.sem, 1)
                d_e.wait(dve, b, n + 1)
                V.reciprocal(wgt[:, s, :], den[:, s, :]).then_inc(d_w.sem, 1)

            def difference(b, n):
                a_d.wait(dve, b, n + 1)
                V.tensor_tensor(dT[:, :], gvT[:, n, :], vT[:, n, :], ALU.subtract).then_inc(d_d.sem, 1)

            def attended(b, n):
                d_d.wait(dve, b, n + 1)
                s_deg.wait(dve, b, n + 1)
                V.tensor_tensor(aT[:, n, :], bank[6][:, 0:TOKENS], dT[:, :], ALU.mult).then_inc(d_a.sem, 1)

            def output_bias(b):
                s_y.wait(dve, b, 1)
                V.tensor_scalar(yT[:, :], bank[7][:, 0:TOKENS], yb[:, :], None, ALU.add).then_inc(d_yT.sem, 1)

            def output_kept(b):
                s_yn.wait(dve, b, 1)
                V.tensor_copy(y_all[:, tokens(b), :],
                              bank[7][:, 0:TOKENS].rearrange("p (t d) -> p t d", t=TILES)).then_inc(d_y.sem, 1)

            def phase1(b, before, tokens_of=None):
                for n in range(PAIRS + 2):
                    if 0 <= n - 1 < PAIRS:
                        adjacency(b, n - 1)
                    if n >= 3:
                        difference(b, n - 3)
                    if n < PAIRS:
                        maxima(b, n, 0)
                    if n >= 3:
                        attended(b, n - 3)
                    if n < PAIRS:
                        maxima(b, n, 1)
                    if n == 2 and before is not None:
                        output_bias(before)
                    if n == 3 and before is not None:
                        output_kept(before)
                    if tokens_of is not None:
                        routing(tokens_of, n)
                    if n >= PAIRS:
                        layer1_out(b, n - PAIRS)
                        if before is not None:
                            norm_tokens(before, n - PAIRS)
                difference(b, PAIRS - 1)
                attended(b, PAIRS - 1)

            def layer1_out(b, n):
                s_f1.wait(dve, b, n + 1)
                V.tensor_tensor(z1[:, n % 2, :], bank[n % 2][:, 0:TOKENS], vT[:, n, :], ALU.add).then_inc(d_z1.sem, 1)

            def layer2_out(b, n):
                s_h2.wait(dve, b, n + 1)
                V.tensor_tensor(z2[:, n % 2, :], bank[4 + n % 2][:, 0:TOKENS], f1T[:, n % 4, :],
                                ALU.add).then_inc(d_z2.sem, 1)

            def phase2(b, before, after):
                for n in range(2, PAIRS + 2):
                    if n < PAIRS:
                        layer1_out(b, n)
                    if n == 8 and after is not None:
                        x_low(after)
                    layer2_out(b, n - 2)
                    if after is not None:
                        norm_step(after, n - 2)
                    else:
                        split_gate_up(n - 2)
                        step_table(n - 2)
                    if before is not None:
                        for i in NORM_STEPS[n - 2]:
                            norm_tokens(before, i)

            NORM_STEPS = ((2, 3), (4, 5), (6,), (7, 8), (9, 10), (), (11,), ())

            def split_gate_up(e):
                dve.wait_ge(w_gu[e % 2], 16 * (e // 2 + 1))
                V.tensor_copy(gu_hi[:, e, :], raw_gu[:, e % 2, :]).then_inc(k_gu, 1)
                dve.wait_ge(k_gu, 2 * e + 1)
                V.tensor_tensor(gu_lo[:, e, :], raw_gu[:, e % 2, :], gu_hi[:, e, :].bitcast(f32),
                                ALU.subtract).then_inc(k_gu, 1)

            class Steps:

                def __init__(self, steps, turn, n):
                    self.steps, self.turn, self.n = steps, turn, n

                def done(self, ins):
                    self.n += 1
                    ins.then_inc(self.steps.sem, 1)

                def ready(self):
                    self.steps.wait(dve, self.turn, self.n)

                def ready_ahead(self):
                    wait_ahead(self.steps, self.turn, self.n)

            def norm_tokens(p, step):
                now = tokens(p)
                x1 = x_all[:, now, :]

                def tile(whole, t):
                    return whole[:, bass.ds(p * TILES + t, 1), :].rearrange("p o d -> p (o d)")

                def moments(src, s):
                    if s.n:
                        s.ready_ahead()
                    for t in range(TILES):
                        last = V.bn_stats(st4[:, t, :], tile(src, t))
                    s.done(last)

                def variances(s):
                    s.ready_ahead()
                    for t in range(TILES):
                        last = V.bn_aggr(mv4[:, t, :], st4[:, t, :])
                    s.done(last)
                    s.ready()
                    s.done(V.tensor_scalar(ve4[:, :], mv4[:, :, 1], EPS_LN, None, ALU.add))

                def normalised(src, s, power):
                    p_st.wait(dve, p, power)
                    for t in range(TILES):
                        last = V.tensor_scalar(t4[:, t, :], tile(src, t), mv4[:, t, 0:1], rs4[:, t:t + 1],
                                               ALU.subtract, ALU.mult)
                    s.done(last)

                if step == 0:
                    d_y.wait(dve, p, 1)
                    V.memset(hold[:, :], 0.0)
                    moments(y_all, Steps(d_st, p, 0))
                elif step == 1:
                    variances(Steps(d_st, p, 1))
                elif step == 2:
                    normalised(y_all, Steps(d_st, p, 3), 1)
                elif step == 3:
                    s = Steps(d_st, p, 4)
                    s.ready()
                    s.done(V.tensor_tensor(t4[:, :, :], t4[:, :, :],
                                           gout[:, :].unsqueeze(1).to_broadcast([P, TILES, DIM]), ALU.mult))
                elif step == 4:
                    s = Steps(d_st, p, 5)
                    s.ready()
                    s.done(V.tensor_tensor(x1, x1, t4[:, :, :], ALU.add))
                elif step == 5:
                    moments(x_all, Steps(d_st, p, 6))
                elif step == 6:
                    variances(Steps(d_st, p, 7))
                elif step == 7:
                    normalised(x_all, Steps(d_st, p, 9), 2)
                elif step == 8:
                    s = Steps(d_st, p, 10)
                    s.ready()
                    s.done(V.tensor_tensor(x1, x1, t4[:, :, :], ALU.add))
                elif step == 9:
                    s = Steps(d_st, p, 11)
                    for t in range(TILES):
                        last = V.scalar_tensor_tensor(sq4[:, t, :], t4[:, t, :], 1.0, t4[:, t, :], ALU.mult,
                                                      ALU.mult, accum_out=ss4[:, t:t + 1])
                    s.done(last)
                elif step == 10:
                    s = Steps(d_st, p, 12)
                    s.ready()
                    s.done(V.tensor_scalar(ve4[:, :], ss4[:, :], 1.0 / DIM, EPS_RMS, ALU.mult, ALU.add))
                elif step == 11:
                    p_st.wait(dve, p, 3)
                    s = Steps(d_st, p, 13)
                    for t in range(TILES):
                        last = V.tensor_scalar(z4[:, t, :], t4[:, t, :], rs4[:, t:t + 1], None, ALU.mult)
                    s.done(last)
                    assert s.n == NORMED

            def choose(p, part, o=None):
                if part == 0:
                    s_lg.wait(dve, p, 1)
                    s = Steps(d_ch, p, 0)
                    s.done(V.tensor_copy(lg[:, :, :], o[:, LOGITS].rearrange("p (t e) -> p t e", t=TILES)))
                    s.ready_ahead()
                    for t in range(TILES):
                        last = V.max(top[:, t, :], lg[:, t, :])
                    s.done(last)
                    s.ready()
                    s.done(V.tensor_tensor(gap[:, :], top[:, :, 0], top[:, :, 1], ALU.subtract))
                elif part == 1:
                    s = Steps(d_ch, p, 3)
                    for t in range(TILES):
                        last = V.max_index(topi[:, t, :], top[:, t, :], lg[:, t, :])
                    s.done(last)
                    s.ready()
                    s.done(V.tensor_copy(topf[:, :, :], topi[:, :, 0:CHOICES]))
                    s.ready()
                    for r in range(CHOICES):
                        last = V.tensor_tensor(eq[:, r, :, :], iot[:, :].unsqueeze(1).to_broadcast([P, TILES, EXPERTS]),
                                               topf[:, :, r:r + 1].to_broadcast([P, TILES, EXPERTS]), ALU.is_equal)
                    s.done(last)
                    s.ready()
                    s.done(V.tensor_copy(eq_bf[:, 0:SIDE, :], eq[:, :, :, :].rearrange("p r t e -> p (r t) e")))
                    assert s.n == ONE_HOT
                else:
                    def w(r):
                        return share[:, bass.ds(p, 1), r, :].rearrange("p o t -> p (o t)")
                    a_ratio.wait(dve, p, 1)
                    s = Steps(d_ch, p, 7)
                    s.done(V.tensor_scalar(ratio1[:, :], ratio[:, :], 1.0, None, ALU.add))
                    s.ready()
                    s.done(V.reciprocal(ratio1[:, :], ratio1[:, :]))
                    s.ready()
                    s.done(V.tensor_scalar(w(0), ratio1[:, :], alph[:, :], None, ALU.mult))
                    s.ready()
                    s.done(V.tensor_tensor(w(1), w(0), ratio[:, :], ALU.mult))
                    assert s.n == d_ch.per

            def place_tokens(p):
                s_pre.wait(dve, p, 1)
                pre = bank[7][:, PLACES].rearrange("p (c e) -> p c e", e=EXPERTS)
                s = Steps(d_pl, p, 0)
                s.done(V.tensor_tensor(place[:, :, :], pre[:, 0:SIDE, :],
                                       next_row[:, :].unsqueeze(1).to_broadcast([P, SIDE, EXPERTS]), ALU.add))
                s.ready()
                s.done(V.tensor_tensor(place[:, :, :], place[:, :, :],
                                       eq[:, :, :, :].rearrange("p r t e -> p (r t) e"), ALU.mult))
                s.done(V.tensor_tensor(next_row[:, :], next_row[:, :], pre[:, SIDE, :], ALU.add))
                s.ready()
                s.done(V.tensor_reduce(row_f[:, :], place[:, :, :], X, ALU.add))
                s.ready()
                s.done(V.tensor_copy(row_all[:, bass.ds(p, 1), :].rearrange("p o c -> p (o c)"), row_f[:, :]))
                s.done(V.tensor_copy(row_now[:, :], row_f[:, :]))
                assert s.n == d_pl.per

            def routing(p, n):
                if n in (1, 2):
                    choose(p, n - 1, bank[6])
                if n == 3:
                    choose(p, 2)
                if n == 5:
                    place_tokens(p)

            def step_table(i):
                each = [P, STEPS, EXPERTS]

                def then(ins):
                    ins.then_inc(d_tab, 1)

                if i == 0:
                    d_pl.wait(dve, SORTED, 0)
                    then(V.tensor_tensor(used[:, :], next_row[:, :], first_row[:, :], ALU.subtract))
                    dve.wait_ge(d_tab, 1)
                    then(V.tensor_tensor(taken[:, :, :], used[:, :].unsqueeze(2).to_broadcast([P, EXPERTS, ROOM]),
                                         tile_from[:, :].unsqueeze(1).to_broadcast([P, EXPERTS, ROOM]), ALU.is_gt))
                    dve.wait_ge(d_tab, 2)
                    then(V.tensor_reduce(tiles_used[:, :], taken[:, :, :], X, ALU.add))
                if i == 1:
                    dve.wait_ge(d_tab, 3)
                    V.tensor_scalar(unused[:, :], tiles_used[:, :], -1.0, float(ROOM), ALU.mult, ALU.add)
                    then(V.tensor_tensor(passed_by[:, :, :], upto[:, :, :],
                                         tiles_used[:, :].unsqueeze(1).to_broadcast([P, EXPERTS, EXPERTS]), ALU.mult))
                    dve.wait_ge(d_tab, 4)
                    then(V.tensor_reduce(last_step[:, :], passed_by[:, :, :], X, ALU.add))
                if i == 2:
                    dve.wait_ge(d_tab, 5)
                    then(V.tensor_tensor(passed[:, :, :], last_step[:, :].unsqueeze(1).to_broadcast(each),
                                         step_no[:, :].unsqueeze(2).to_broadcast(each), ALU.is_le))
                if i == 3:
                    dve.wait_ge(d_tab, 6)
                    then(V.tensor_reduce(step_f[:, 0, :], passed[:, :, :], X, ALU.add))
                    dve.wait_ge(d_tab, 7)
                    then(V.tensor_scalar(step_expert[:, :], step_f[:, 0, :], float(EXPERTS - 1), None, ALU.min))
                if i == 4:
                    then(V.tensor_tensor(passed[:, :, :], passed[:, :, :],
                                         unused[:, :].unsqueeze(1).to_broadcast(each), ALU.mult))
                    dve.wait_ge(d_tab, 9)
                    then(V.tensor_reduce(step_f[:, 1, :], passed[:, :, :], X, ALU.add))
                if i == 5:
                    dve.wait_ge(d_tab, 10)
                    V.tensor_tensor(step_f[:, 1, :], step_f[:, 1, :], step_no[:, :], ALU.add).then_inc(k_row, 1)
                    dve.wait_ge(k_row, 1)
                    then(V.tensor_scalar(step_row[:, :], step_f[:, 1, :], float(P), None, ALU.mult))

            def slots_low(g, i):
                if not live(g, i):
                    return
                a_zh.wait(dve, step(g, i), 1)
                V.scalar_tensor_tensor(sz_lo[:, i % 2, :], bank[4][:, 0:P], normw[:, :],
                                       sz_hi[:, i % 2, :].bitcast(f32), ALU.mult, ALU.subtract).then_inc(d_zlo.sem, 1)

            def sorted_hidden(g, i):
                if not live(g, i):
                    return
                s_gu.wait(dve, 2 * step(g, i), 2)
                a_silu.wait(dve, step(g, i), 1)
                if live(g, i - 2):
                    s_ht.wait(dve, step(g, i - 2), 1)
                V.tensor_tensor(shid[:, i % 2, 0:HID], bank[2 + i % 2][:, 0:HID], ssg[:, i % 2, :],
                                ALU.mult).then_inc(d_hid.sem, 1)

            def slots_out(g, i):
                if not live(g, i):
                    return
                q, s = turn(g, i)
                s_down.wait(dve, step(g, i), 1)
                if live(g, i - UNROLL):
                    w_zout[s].wait(dve, q, 0)
                V.tensor_copy(zout[:, s, :], bank[7][:, 0:DIM]).then_inc(d_zout.sem, 1)

            def kept_split(p):
                m = p - SORTED
                cols = slice(m * TOKENS, (m + 1) * TOKENS)
                a_zt.wait(dve, p, 1)
                V.tensor_copy(zt[:, 0, cols], zT[:, :]).then_inc(d_zt, 1)
                dve.wait_ge(d_zt, 2 * m + 1)
                V.tensor_tensor(zt[:, 1, cols], zT[:, :], zt[:, 0, cols].bitcast(f32), ALU.subtract).then_inc(d_zt, 1)

            def kept_weights(p):
                m = p - SORTED
                d_ch.wait(dve, p, d_ch.per)
                for r in range(CHOICES):
                    last = V.tensor_tensor(eq[:, r, :, :], eq[:, r, :, :],
                                           share[:, p, r, :].unsqueeze(2).to_broadcast([P, TILES, EXPERTS]), ALU.mult)
                last.then_inc(k_eq, 1)
                dve.wait_ge(k_eq, m + 1)
                V.tensor_tensor(comb[:, m * TILES:(m + 1) * TILES, :], eq[:, 0, :, :], eq[:, 1, :, :],
                                ALU.add).then_inc(d_comb, 1)

            def sorted_group(g):
                for i in range(UNROLL):
                    sorted_hidden(g, i)
                    if isinstance(g, int) and step(g, i) == 1:
                        choose(BATCHES - 2, 0, bank[4])
                    if isinstance(g, int) and step(g, i) == KEPT_Z + 1:
                        choose(BATCHES - 1, 0, bank[4])
                    slots_low(g, i + 2)
                    if isinstance(g, int) and g == 0 and i == 0:
                        output_kept(BATCHES - 1)
                    slots_out(g, i - 2)
                    if isinstance(g, int):
                        j = step(g, i)
                        p = BATCHES - 2
                        if j == 2:
                            kept_split(p)
                            choose(p, 1)
                        if j == 6:
                            choose(p, 2)
                            kept_weights(p)
                        p = BATCHES - 1
                        if 2 <= j < 8:
                            for k in (2 * j - 4, 2 * j - 3):
                                norm_tokens(p, k)
                        if j == KEPT_Z + 2:
                            kept_split(p)
                        if j == KEPT_Z + 3:
                            choose(p, 1)

            def sorted_stage():
                V.memset(shid[:, :, HID:], 0.0)
                slots_low(0, 0)
                slots_low(0, 1)
                output_bias(BATCHES - 1)
                for g in range(2):
                    sorted_group(g)
                with dve.Fori(2, GROUPS - 1) as g:
                    sorted_group(g)
                sorted_group(GROUPS - 1)
                p = BATCHES - 1
                slots_out(GROUPS, -2)
                choose(p, 2)
                slots_out(GROUPS, -1)
                kept_weights(p)

            def hidden(i):
                e, c = i // NC, i % NC
                n = CHUNKS[c][1]
                dve.wait_ge(a_sg, i + 1)
                dve.wait_ge(s_up, i + 1)
                if c == 0 and e >= 2:
                    dve.wait_ge(s_dn, e - 1)
                V.tensor_tensor(hT[0:n, e % 2, c, :], bank[2 + i % 2][0:n, :], sg[0:n, i % 2, :],
                                ALU.mult).then_inc(d_h, 1)

            def add_expert(e):
                dve.wait_ge(s_dn, e + 1)
                if e > 0:
                    dve.wait_ge(d_acc, e)
                for t in range(BT):
                    src = x_all[:, ROOM + t, :] if e == 0 else acc[:, t, :]
                    last = V.scalar_tensor_tensor(acc[:, t, :], bank[4 + e % 2][:, xt(t)], comb[:, t, e:e + 1], src,
                                                  ALU.mult, ALU.add)
                last.then_inc(d_acc, 1)

            def finish(q):
                dve.wait_ge(w_got[q % UNROLL], 2 * 16 * (q // UNROLL + 1))
                b, t = q // TILES, q % TILES
                for r in range(CHOICES):
                    if r > 0:
                        dve.wait_ge(d_fin, 2 * q + r)
                    V.scalar_tensor_tensor(x_all[:, q, :], got[:, q % UNROLL, r, :], share[:, b, r, t:t + 1],
                                           x_all[:, q, :], ALU.mult, ALU.add).then_inc(d_fin, 1)

            def every_expert():
                q = 0
                for i in range(EXPERTS * NC):
                    hidden(i)
                    if i % NC == 1 and i > NC:
                        add_expert(i // NC - 1)
                    if i >= 3:
                        finish(q)
                        q += 1
                add_expert(EXPERTS - 1)
                for q in range(q, ROOM):
                    finish(q)

            dve.wait_ge(w_x0, 16)
            for i in range(6):
                norm_step(0, i)
            prepare_weights()
            x_low(0)
            phase1(0, None)
            dve.wait_ge(w_x, 16)
            phase2(0, None, 1)
            phase1(1, 0)
            with dve.Fori(1, BATCHES - 2) as b:
                phase2(b, b - 1, b + 1)
                phase1(b + 1, b, b - 1)
            phase2(BATCHES - 2, BATCHES - 3, BATCHES - 1)
            phase1(BATCHES - 1, BATCHES - 2, BATCHES - 3)
            phase2(BATCHES - 1, BATCHES - 2, None)
            sorted_stage()
            every_expert()


def kernel(**inputs):
    import numpy as np
    import concourse.bacc as bacc
    from concourse.bass_utils import run_bass_kernel_spmd

    a = {n[3:]: np.asarray(v) for n, v in inputs.items()}
    given = dict(
        x=a["attn_x"].reshape(ALL, DIM), wq=a["attn_Wq"], wk=a["attn_Wk"], wv=a["attn_Wv"],
        wvT=a["attn_Wv"].T, gnn_w=a["attn_gnn_w"], gnn_b=a["attn_gnn_b"], lin_wT=a["attn_lin_w"].T,
        lin_b=a["attn_lin_b"].reshape(DHEAD, 1), wo=a["attn_Wo"], gamma_in=a["attn_gamma_in"].reshape(DIM, 1),
        gamma_out=a["attn_gamma_out"].reshape(1, DIM), norm_w=a["ffn_norm_weight"].reshape(DIM, 1),
        routerT=a["ffn_router_weight"].T, guT=a["ffn_gate_up_weight"].transpose(0, 2, 1),
        downT=a["ffn_down_weight"].transpose(0, 2, 1), alpha=a["ffn_residual_alpha"].reshape(1, 1))
    given = {n: np.ascontiguousarray(v) for n, v in given.items()}
    nc = bacc.Bacc("TRN2", target_bir_lowering=False, num_devices=1)
    args = {n: nc.dram_tensor(f"in_{n}", v.shape, f32, kind="ExternalInput").ap() for n, v in given.items()}
    slots = nc.dram_tensor("slots", (SLOT_ROWS, DIM), f32, kind="Internal").ap()
    out = nc.dram_tensor("out", (ALL, DIM), f32, kind="ExternalOutput").ap()
    build_program(nc, slots=slots, out=out, **args)
    r = run_bass_kernel_spmd(nc, [{f"in_{n}": v for n, v in given.items()}], core_ids=[0])
    return r.results[0]["out"].reshape(BATCHES, TOKENS, DIM)
```
